# Optimizing a Trainium2 kernel written in Bass

```python
import numpy as np
import jax
import jax.numpy as jnp

def _softmax(x, axis=-1):
    return jax.nn.softmax(x, axis=axis)

def _gelu(x):
    return jax.nn.gelu(x, approximate=True)

def _silu(x):
    return jax.nn.silu(x)

def _sigmoid(x):
    return jax.nn.sigmoid(x)

def _layernorm(x, axis=-1, eps=1e-05):
    m = jnp.mean(x, axis=axis, keepdims=True)
    v = jnp.var(x, axis=axis, keepdims=True)
    return (x - m) / jnp.sqrt(v + eps)

def _scatter_add(tgt, idx, src, axis=0):
    return tgt.at[idx].add(src)

def _segment_sum(src, seg, n):
    return jax.ops.segment_sum(src, seg, n)
kernel_name = 'mk_adaln_d1_jaxref_r8_11a09c'

def setup_inputs(seed: int=0):
    np.random.seed(seed)
    _w = jnp.asarray

    def _L0_attn_setup():
        import jax, jax.numpy as jnp
        import numpy as np
        NUM_HEADS = 16
        EMBED_DIM = 128

        def _linear_attention(x, Wq, bq, Wk, bk, Wv, bv, Wo, bo):
            B, S, D = x.shape
            H = NUM_HEADS
            hd = D // H
            v = (x @ Wv + bv).reshape(B, S, H, hd)
            q = (x @ Wq + bq).reshape(B, S, H, hd)
            k = (x @ Wk + bk).reshape(B, S, H, hd)
            q = jax.nn.elu(q) + 1.0
            k = jax.nn.elu(k) + 1.0
            qT = q.transpose(1, 0, 2, 3)
            kT = k.transpose(1, 0, 2, 3)
            vT = v.transpose(1, 0, 2, 3)
            s0 = jnp.zeros((B, H, hd, hd), dtype=x.dtype)
            z0 = jnp.zeros((B, H, hd), dtype=x.dtype)

            def step(carry, qkv):
                s, z = carry
                q_i, k_i, v_i = qkv
                s = s + jnp.einsum('bhd,bhm->bhdm', k_i, v_i)
                z = z + k_i
                qs = jnp.einsum('bhd,bhdm->bhm', q_i, s)
                qz = jnp.einsum('bhd,bhd->bh', q_i, z)[..., None]
                return ((s, z), qs / (qz + 1e-06))
            (_, _), values = jax.lax.scan(step, (s0, z0), (qT, kT, vT))
            values = values.transpose(1, 0, 2, 3).reshape(B, S, D)
            return values @ Wo + bo
        key = jax.random.key(seed)
        ks = jax.random.split(key, 6)
        B, S, D = (4, 256, EMBED_DIM)
        sc = 1.0 / np.sqrt(D)
        return {'x': jax.random.normal(ks[0], (B, S, D), dtype=jnp.float32), 'mask': jnp.ones((B, S), dtype=jnp.int32), 'Wq': jax.random.normal(ks[1], (D, D), dtype=jnp.float32) * sc, 'bq': jnp.zeros((D,), dtype=jnp.float32), 'Wk': jax.random.normal(ks[2], (D, D), dtype=jnp.float32) * sc, 'bk': jnp.zeros((D,), dtype=jnp.float32), 'Wv': jax.random.normal(ks[3], (D, D), dtype=jnp.float32) * sc, 'bv': jnp.zeros((D,), dtype=jnp.float32), 'Wo': jax.random.normal(ks[4], (D, D), dtype=jnp.float32) * sc, 'bo': jnp.zeros((D,), dtype=jnp.float32)}
    _L0_attn_in = _L0_attn_setup()

    def _L0_ffn_setup():
        import jax, jax.numpy as jnp
        import numpy as np
        H = 128
        I = 64
        E = 8
        K = 2
        SI = I * 2
        B, S = (2, 128)

        def _mlp(x, gw, uw, dw):
            return jax.nn.silu(x @ gw.T) * (x @ uw.T) @ dw.T
        key = jax.random.key(seed)
        ks = jax.random.split(key, 9)
        s = 0.02
        return {'x': jax.random.normal(ks[0], (B, S, H), jnp.float32), 'gate_w': jax.random.normal(ks[1], (E, H), jnp.float32) * s, 'lb_bias': jnp.zeros((E,), jnp.float32), 'expert_gate_w': jax.random.normal(ks[2], (E, I, H), jnp.float32) * s, 'expert_up_w': jax.random.normal(ks[3], (E, I, H), jnp.float32) * s, 'expert_down_w': jax.random.normal(ks[4], (E, H, I), jnp.float32) * s, 'shared_gate_w': jax.random.normal(ks[5], (SI, H), jnp.float32) * s, 'shared_up_w': jax.random.normal(ks[6], (SI, H), jnp.float32) * s, 'shared_down_w': jax.random.normal(ks[7], (H, SI), jnp.float32) * s}
    _L0_ffn_in = _L0_ffn_setup()
    _L0_c = _w((lambda *s: np.random.randn(*s).astype(np.float32) * 0.05)(8, 128))
    _L0_wmod = _w((lambda *s: np.random.randn(*s).astype(np.float32) * 0.05)(128, 6 * 128) * 128 ** (-0.5))
    _d = {'L0_attn_x': _L0_attn_in['x'], 'L0_attn_mask': _L0_attn_in['mask'], 'L0_attn_Wq': _L0_attn_in['Wq'], 'L0_attn_bq': _L0_attn_in['bq'], 'L0_attn_Wk': _L0_attn_in['Wk'], 'L0_attn_bk': _L0_attn_in['bk'], 'L0_attn_Wv': _L0_attn_in['Wv'], 'L0_attn_bv': _L0_attn_in['bv'], 'L0_attn_Wo': _L0_attn_in['Wo'], 'L0_attn_bo': _L0_attn_in['bo'], 'L0_ffn_gate_w': _L0_ffn_in['gate_w'], 'L0_ffn_lb_bias': _L0_ffn_in['lb_bias'], 'L0_ffn_expert_gate_w': _L0_ffn_in['expert_gate_w'], 'L0_ffn_expert_up_w': _L0_ffn_in['expert_up_w'], 'L0_ffn_expert_down_w': _L0_ffn_in['expert_down_w'], 'L0_ffn_shared_gate_w': _L0_ffn_in['shared_gate_w'], 'L0_ffn_shared_up_w': _L0_ffn_in['shared_up_w'], 'L0_ffn_shared_down_w': _L0_ffn_in['shared_down_w'], 'L0_c': _L0_c, 'L0_wmod': _L0_wmod}
    _x0 = _d['L0_attn_x']
    _d['L0_attn_x'] = jax.random.normal(jax.random.fold_in(jax.random.key(seed), 1), (8, 1024, 128), dtype=_x0.dtype)
    del _x0
    return _d

def reference(L0_attn_x, L0_attn_mask, L0_attn_Wq, L0_attn_bq, L0_attn_Wk, L0_attn_bk, L0_attn_Wv, L0_attn_bv, L0_attn_Wo, L0_attn_bo, L0_ffn_gate_w, L0_ffn_lb_bias, L0_ffn_expert_gate_w, L0_ffn_expert_up_w, L0_ffn_expert_down_w, L0_ffn_shared_gate_w, L0_ffn_shared_up_w, L0_ffn_shared_down_w, L0_c, L0_wmod):

    def _L0_attn_ref(x, mask, Wq, bq, Wk, bk, Wv, bv, Wo, bo):
        import jax, jax.numpy as jnp
        import numpy as np
        NUM_HEADS = 16
        EMBED_DIM = 128

        def _linear_attention(x, Wq, bq, Wk, bk, Wv, bv, Wo, bo):
            B, S, D = x.shape
            H = NUM_HEADS
            hd = D // H
            v = (x @ Wv + bv).reshape(B, S, H, hd)
            q = (x @ Wq + bq).reshape(B, S, H, hd)
            k = (x @ Wk + bk).reshape(B, S, H, hd)
            q = jax.nn.elu(q) + 1.0
            k = jax.nn.elu(k) + 1.0
            qT = q.transpose(1, 0, 2, 3)
            kT = k.transpose(1, 0, 2, 3)
            vT = v.transpose(1, 0, 2, 3)
            s0 = jnp.zeros((B, H, hd, hd), dtype=x.dtype)
            z0 = jnp.zeros((B, H, hd), dtype=x.dtype)

            def step(carry, qkv):
                s, z = carry
                q_i, k_i, v_i = qkv
                s = s + jnp.einsum('bhd,bhm->bhdm', k_i, v_i)
                z = z + k_i
                qs = jnp.einsum('bhd,bhdm->bhm', q_i, s)
                qz = jnp.einsum('bhd,bhd->bh', q_i, z)[..., None]
                return ((s, z), qs / (qz + 1e-06))
            (_, _), values = jax.lax.scan(step, (s0, z0), (qT, kT, vT))
            values = values.transpose(1, 0, 2, 3).reshape(B, S, D)
            return values @ Wo + bo
        return _linear_attention(x, Wq, bq, Wk, bk, Wv, bv, Wo, bo)

    def _L0_ffn_ref(x, gate_w, lb_bias, expert_gate_w, expert_up_w, expert_down_w, shared_gate_w, shared_up_w, shared_down_w):
        import jax, jax.numpy as jnp
        import numpy as np
        H = 128
        I = 64
        E = 8
        K = 2
        SI = I * 2
        B, S = (2, 128)

        def _mlp(x, gw, uw, dw):
            return jax.nn.silu(x @ gw.T) * (x @ uw.T) @ dw.T
        b, s, h = x.shape
        xf = x.reshape(-1, h)
        logits = xf @ gate_w.T + lb_bias
        scores = jax.nn.sigmoid(logits.astype(jnp.float32))
        topw, topi = jax.lax.top_k(scores, K)
        topw = (topw / (topw.sum(-1, keepdims=True) + 1e-08)).astype(x.dtype)
        out = jnp.zeros_like(xf)
        for e in range(E):
            m = topi == e
            sel = m.any(axis=-1)
            cnt = m.sum()
            wmean = (topw * m).sum() / jnp.maximum(cnt, 1).astype(topw.dtype)
            y = _mlp(xf, expert_gate_w[e], expert_up_w[e], expert_down_w[e])
            out = out + jnp.where(sel[:, None], y * wmean, jnp.zeros((), x.dtype))
        out = out.reshape(b, s, h)
        out = out + _mlp(x, shared_gate_w, shared_up_w, shared_down_w)
        return out
    x = L0_attn_x
    mod = (_silu(L0_c) @ L0_wmod).reshape(L0_c.shape[0], 6, 1, -1)
    sa, ca, ga, sb, cb, gb = (mod[:, 0], mod[:, 1], mod[:, 2], mod[:, 3], mod[:, 4], mod[:, 5])
    ga = (2 * (ga >= 0) - 1) * jnp.maximum(jnp.abs(ga), 0.25)
    gb = (2 * (gb >= 0) - 1) * jnp.maximum(jnp.abs(gb), 0.25)
    h = _layernorm(x, axis=-1) * (1 + ca) + sa
    x = x + ga * _L0_attn_ref(h, L0_attn_mask, L0_attn_Wq, L0_attn_bq, L0_attn_Wk, L0_attn_bk, L0_attn_Wv, L0_attn_bv, L0_attn_Wo, L0_attn_bo)
    h = _layernorm(x, axis=-1) * (1 + cb) + sb
    x = x + gb * _L0_ffn_ref(h, L0_ffn_gate_w, L0_ffn_lb_bias, L0_ffn_expert_gate_w, L0_ffn_expert_up_w, L0_ffn_expert_down_w, L0_ffn_shared_gate_w, L0_ffn_shared_up_w, L0_ffn_shared_down_w)
    return x

_drawn_inputs = setup_inputs


def setup_inputs(seed=0):
    import zlib

    import numpy as np

    out = dict(_drawn_inputs(seed))
    spreads = {'L0_attn_bq': (0.0, 0.8),
     'L0_attn_bk': (0.0, 0.8),
     'L0_attn_bv': (0.0, 0.341),
     'L0_attn_bo': (0.0, 0.324),
     'L0_ffn_lb_bias': (0.0, 0.8)}
    factors = {'L0_attn_Wq': 8.0,
     'L0_attn_Wk': 6.894,
     'L0_ffn_gate_w': 8.0,
     'L0_ffn_expert_gate_w': 8.0,
     'L0_ffn_expert_up_w': 8.0,
     'L0_ffn_expert_down_w': 8.0,
     'L0_ffn_shared_gate_w': 8.0,
     'L0_ffn_shared_up_w': 8.0,
     'L0_ffn_shared_down_w': 8.0}
    for name, (base, spread) in spreads.items():
        noise = np.random.default_rng([zlib.crc32(name.encode()), seed]).standard_normal(out[name].shape)
        drawn = base * np.exp(spread * noise) if base else spread * noise
        out[name] = jnp.asarray(drawn.astype(out[name].dtype))
    for name, factor in factors.items():
        out[name] = (out[name] * factor).astype(out[name].dtype)
    return out
```

```python
from contextlib import ExitStack

import concourse.bass as bass
from concourse import mybir

F32 = mybir.dt.float32
BF16 = mybir.dt.bfloat16
ALU = mybir.AluOpType
ACT = mybir.ActivationFunctionType
AX_X = mybir.AxisListType.X
ts = bass.ts

P = 128
CPB = 8
HEADS, HD = 16, 8
HV = HD + 1
FV = HEADS * HV
KVW = HEADS * HD * HV
THIRDS = [(0, 6), (6, 11), (11, 16)]
UNITS = 5
MASKED_OUT = -1.0e30
LN_EPS = 1e-5


def at(b, c, lag):
    while lag > c:
        b, c = b - 1, c + CPB
    return b, c - lag, b * CPB + (c - lag)


def adaln_block(nc, x_in, wq, bq, wk, bk, wv, bv, wo, bo, gate_w, lb_bias, eg_w, eu_w, ed_w,
                sg_w, su_w, sd_w, cond, wmod, out):
    B, S, D = x_in.shape
    E, I, _ = eg_w.shape
    NCH = B * S // P
    assert D == P and S == CPB * P and E * I == (UNITS - 1) * P and D == HEADS * HD
    XCH = NCH + 2
    TILES = B * 2

    with ExitStack() as ctx:
        def sb(name, shape, dt=F32):
            return ctx.enter_context(nc.sbuf_tensor(name, shape, dt))

        def bank(name):
            return ctx.enter_context(nc.psum_tensor(name, [P, 512], F32))

        def sem(name):
            return ctx.enter_context(nc.semaphore(name))

        x_all = sb("x_all", [P, XCH * P])
        h2T_all = sb("h2T_all", [P, NCH * P])
        w_qkv = sb("w_qkv", [P, 3 * P])
        w_o = sb("w_o", [P, P])
        w_o_ga = sb("w_o_ga", [P, P])
        wmod_sb = sb("wmod_sb", [P, 6 * D])
        cond_sb = sb("cond_sb", [B, D])
        condT = sb("condT", [P, 3, B])
        condT_b = sb("condT_b", [P, B, P])
        modT = sb("modT", [P, 6, B])
        mod1 = sb("mod1", [P, 2])
        mod2 = sb("mod2", [P, 2])
        ga_bc = sb("ga_bc", [P, B * D])
        gb_bc = sb("gb_bc", [P, B * D])
        sgn_bc = sb("sgn_bc", [P, B * D])
        lb_bc = sb("lb_bc", [P, E])
        raw_g = sb("raw_g", [P, UNITS, D])
        raw_u = sb("raw_u", [P, UNITS, D])
        raw_d = sb("raw_d", [P, UNITS * P])
        raw_r = sb("raw_r", [E, D])
        gwT = sb("gwT", [P, UNITS, P])
        uwT = sb("uwT", [P, UNITS, P])
        dwT = sb("dwT", [P, UNITS, P])
        rwT = sb("rwT", [P, E])
        ident = sb("ident", [P, P])
        ident_b = sb("ident_b", [P, P], BF16)
        tri = sb("tri", [P, P])
        head_mask = sb("head_mask", [P, FV])
        pick = sb("pick", [E, UNITS - 1, 2, I], BF16)
        ones_b = sb("ones_b", [P, P], BF16)
        ones_f = sb("ones_f", [P, P])
        neg1 = sb("neg1", [P, 1])
        order = sb("order", [P, E])
        bias_row = sb("bias_row", [1, 3 * P])
        bo_row = sb("bo_row", [1, P])
        rest = sb("rest", [1, B * D])
        bias_parts = sb("bias_parts", [P, 3 * P], BF16)
        gabo_row = sb("gabo_row", [1, B * D])
        gabo_parts = sb("gabo_parts", [P, B * D], BF16)

        st = sb("st", [P, 4, 6])
        agg = sb("agg", [P, 4, 2])
        ve = sb("ve", [P, 4])
        lnv = sb("lnv", [P, 4])
        y0 = sb("y0", [P, 4])
        nt1 = sb("nt1", [P, 4])
        nt2 = sb("nt2", [P, 4])
        rstd = sb("rstd", [P, 2, 4])
        nmr = sb("nmr", [P, 2, 4])
        xn = sb("xn", [P, 2, P])
        xn2 = sb("xn2", [P, 2, P])
        hT = sb("hT", [P, 2, P])
        h2T_w = sb("h2T_w", [P, CPB, P])
        e_qk = sb("e_qk", [P, 2, 2 * P])
        qk = sb("qk", [P, 4, 2 * P])
        v_aug = sb("v_aug", [P, 4, HEADS, HV])
        kv = sb("kv", [P, 2, KVW])
        qT = sb("qT", [P, 2, P])
        s_bd = sb("s_bd", [P, 2, FV])
        prod = sb("prod", [P, KVW])
        red = sb("red", [P, FV])
        nd = sb("nd", [P, FV])
        den = sb("den", [P, HEADS])
        rec = sb("rec", [P, HEADS])
        val = sb("val", [P, 2, P])
        valT = sb("valT", [P, 2, P])

        logits = sb("logits", [P, NCH * E])
        gl = [sb(f"gl{i}", [P, NCH * E]) for i in range(6)]
        gm = sb("gm", [P, 6, NCH])
        sel_m1 = sb("sel_m1", [P, NCH * E], BF16)
        sel_w = sb("sel_w", [P, CPB * E], BF16)
        selT = sb("selT", [E, NCH * P], BF16)
        tot = sb("tot", [P, 2 * E])
        wmean = sb("wmean", [P, 3, E])
        silu_g = sb("silu_g", [P, 2, 512])
        hid = sb("hid", [P, 2, 512])
        ffn = sb("ffn", [P, 512])

        ps_t = bank("ps_t")
        ps_a = bank("ps_a")
        ps_q = bank("ps_q")
        ps_i = bank("ps_i")
        ps_s = bank("ps_s")
        ps_c = [bank(f"ps_c{k}") for k in range(3)]
        ps_g = [ps_t, ps_a]
        ps_u = [ps_q, ps_i]
        ps_o = [ps_s, ps_c[0]]

        x_loaded = [sem(f"x_loaded{b}") for b in range(B)]
        w_loaded = sem("w_loaded")
        w2_loaded = sem("w2_loaded")
        out_stored = sem("out_stored")
        names = """const_ident const_all dve_const setup_pe setup_act setup_dve
            xn_done xnT_done hT_done qkv_done v_done exp_done elu_done kv_done C_done qm_done red_done
            qT_ps qT_done ktv_done sbd_done inter_done add_done den_done rec_done norm_done
            valT_ps valT_done y_done x1_done woga_done stat_done agg_done ve_done rs_act newton ln_done
            mod1_done mod2_done xn2_done xn2T_ps h2T_done logits_ps logits_done
            gate_dve gate_act gate_pe selw_done selT_ps selT_done
            g_done u_done silu_done hid_done down_done ffn_done fin_done""".split()
        s = {n: sem(n) for n in names}
        h2T_stored = [sem("h2T_stored0"), sem("h2T_stored1")]

        def split_row(dve, parts, row, n, done, base):
            for k in range(3):
                src = row if k == 0 else rest
                nc.vector.tensor_copy(parts[32 * k:32 * k + 1, 0:n], src[0:1, 0:n]).then_inc(done, 1)
                dve.wait_ge(done, base + 2 * k + 1)
                if k < 2:
                    nc.vector.tensor_copy(hop[0:1, 0:n], parts[32 * k:32 * k + 1, 0:n]).then_inc(done, 1)
                    dve.wait_ge(done, base + 2 * k + 2)
                    nc.vector.tensor_tensor(rest[0:1, 0:n], src[0:1, 0:n], hop[0:1, 0:n],
                                            ALU.subtract).then_inc(s["rest_done"], 1)
                    rest_count[0] += 1
                    dve.wait_ge(s["rest_done"], rest_count[0])

        s["rest_done"] = sem("rest_done")
        rest_count = [0]
        hop = sb("hop", [1, B * D])

        block = ctx.enter_context(nc.Block())

        def pair_par(c):
            return ((c - 1) // 2 + 1) % 2 if c else 0

        def pair_cols(b, c):
            if isinstance(b, int):
                step_no = b * CPB + c
                return (0 if step_no + 2 < NCH else 2), (4 if step_no >= 6 else 2)
            return 0, 4

        def stat_before(pair):
            if isinstance(pair, int):
                return sum(2 if p < 4 or p > NCH // 2 else 4 for p in range(pair))
            return 4 * pair - 8

        def valid(n):
            return not isinstance(n, int) or 0 <= n < NCH

        def wait_count(eng, name, value, cap=None):
            if isinstance(value, int):
                if cap is not None:
                    value = min(value, cap)
                if value <= 0:
                    return
            eng.wait_ge(s[name], value)

        @block.sync
        def _(sp):
            def load(dst, src, done):
                sp.dma_start(dst, src).then_inc(done, 16)

            x_rows = x_in.rearrange("b (c p) d -> b p c d", p=P)
            out_rows = out.rearrange("b (t c p) d -> b t p c d", p=P, c=4)

            def x_batch(b):
                return x_all[:, ts(b, CPB * P)].rearrange("p (c d) -> p c d", d=D)

            load(x_batch(0), x_rows[0], x_loaded[0])
            load(cond_sb[:], cond, w_loaded)
            load(wmod_sb[:], wmod, w_loaded)
            for k, (w, b_) in enumerate(((wq, bq), (wk, bk), (wv, bv))):
                load(w_qkv[:, ts(k, P)], w, w_loaded)
                load(bias_row[0:1, ts(k, P)], b_.rearrange("(a n) -> a n", a=1), w_loaded)
            load(w_o[:], wo, w_loaded)
            load(bo_row[0:1, :], bo.rearrange("(a n) -> a n", a=1), w_loaded)
            load(raw_r[:], gate_w, w2_loaded)
            load(lb_bc[:], lb_bias.rearrange("(a n) -> a n", a=1).to_broadcast([P, E]), w2_loaded)
            for raw, we, ws in ((raw_g, eg_w, sg_w), (raw_u, eu_w, su_w)):
                load(raw[:, 0:UNITS - 1, :], we.rearrange("e i d -> (e i) d").rearrange("(u p) d -> p u d", p=P),
                     w2_loaded)
                load(raw[:, UNITS - 1, :], ws, w2_loaded)
            load(raw_d[:, 0:E * I].rearrange("h (e i) -> h e i", e=E), ed_w.rearrange("e h i -> h e i"), w2_loaded)
            load(raw_d[:, E * I:], sd_w, w2_loaded)

            for b in range(1, B):
                load(x_batch(b), x_rows[b], x_loaded[b])

            def store_h2T(b, half):
                _, _, last = at(b, 4 * half + 3, 0)
                sp.wait_ge(s["h2T_done"], last + 1)
                sp.dma_start(h2T_all[:, bass.ds(b * (CPB * P) + half * 512, 512)],
                             h2T_w[:, 4 * half:4 * half + 4, :]).then_inc(h2T_stored[half], 16)

            with sp.Fori(0, B) as b:
                for half in range(2):
                    store_h2T(b, half)

            with sp.Fori(0, B) as b:
                for t in range(2):
                    sp.wait_ge(s["fin_done"], 2 * b + t + 1)
                    sp.dma_start(out_rows[bass.ds(b, 1), t][0],
                                 x_all[:, bass.ds(b * (CPB * P) + t * 512, 512)]
                                 .rearrange("p (c d) -> p c d", d=D)).then_inc(out_stored, 16)
            for half in range(2):
                sp.wait_ge(h2T_stored[half], 16 * B)
            sp.wait_ge(out_stored, 16 * TILES)

        @block.gpsimd
        def _(pool):
            n = [0]

            def made(ins, wait=True):
                ins.then_inc(s["const_ident"], 1)
                n[0] += 1
                if wait:
                    pool.wait_ge(s["const_ident"], n[0])

            made(nc.gpsimd.memset(ident[:], 0.0))
            made(nc.gpsimd.affine_select(out=ident[:], in_=ident[:], compare_op=ALU.not_equal, fill=1.0,
                                         base=0, pattern=[[-1, P]], channel_multiplier=1))
            made(nc.gpsimd.tensor_copy(ident_b[:], ident[:]))
            made(nc.gpsimd.memset(tri[:], 1.0))
            made(nc.gpsimd.affine_select(out=tri[:], in_=tri[:], compare_op=ALU.is_ge, fill=0.0,
                                         base=0, pattern=[[1, P]], channel_multiplier=-1))
            hm = head_mask[:].rearrange("p (h m) -> p h m", m=HV)
            made(nc.gpsimd.memset(head_mask[:], 1.0))
            made(nc.gpsimd.affine_select(out=hm, in_=hm, compare_op=ALU.is_ge, fill=0.0,
                                         base=0, pattern=[[-HD, HEADS], [0, HV]], channel_multiplier=1))
            made(nc.gpsimd.affine_select(out=hm, in_=hm, compare_op=ALU.is_ge, fill=0.0,
                                         base=HD - 1, pattern=[[HD, HEADS], [0, HV]], channel_multiplier=-1))
            made(nc.gpsimd.memset(pick[:], -MASKED_OUT))
            made(nc.gpsimd.affine_select(out=pick[:], in_=pick[:], compare_op=ALU.is_equal, fill=0.0,
                                         base=0, pattern=[[2, UNITS - 1], [1, 2], [0, I]], channel_multiplier=-1))
            made(nc.gpsimd.iota(order[:], pattern=[[-1, E]], base=E, channel_multiplier=0,
                                allow_small_or_imprecise_dtypes=True))
            made(nc.gpsimd.memset(x_all[:, NCH * P:], 0.0))
            nc.gpsimd.memset(ones_f[:], 1.0).then_inc(s["const_all"], 1)

            def step(b, c):
                _, c2, n2 = at(b, c, 2)
                if not isinstance(n2, int) or 0 <= n2 < NCH:
                    pool.wait_ge(s["elu_done"], n2 + 1)
                    pool.wait_ge(s["v_done"], n2 + 1)
                    if not isinstance(n2, int) or n2 >= 2:
                        pool.wait_ge(s["C_done"], 3 * n2 - 3)
                    k_b = qk[:, c2 % 4, P:2 * P].rearrange("p (h d o) -> p h d o", h=HEADS, o=1)
                    v_b = v_aug[:, c2 % 4].rearrange("p h (o m) -> p h o m", o=1)
                    shape = [P, HEADS, HD, HV]
                    nc.gpsimd.tensor_tensor(kv[:, c2 % 2, :].rearrange("p (h d m) -> p h d m", h=HEADS, d=HD),
                                            k_b.broadcast_to(shape), v_b.broadcast_to(shape),
                                            ALU.mult).then_inc(s["kv_done"], 1)

            for c in range(CPB):
                step(0, c)
            with pool.Fori(1, B) as b:
                for c in range(CPB):
                    step(b, c)
            for c in range(CPB):
                step(B, c)

        @block.tensor
        def _(pe):
            mm = nc.tensor.matmul
            pe.wait_ge(w_loaded, 160)
            pe.wait_ge(s["const_ident"], 2)
            nc.tensor.transpose(ps_t[:, 0:B], cond_sb[:], ident[0:B, 0:B]).then_inc(s["setup_pe"], 1)
            pe.wait_ge(s["setup_dve"], 3)
            for k in range(6):
                last = mm(ps_a[:, k * B:(k + 1) * B], wmod_sb[:, ts(k, D)], condT[:, 2, :], start=True, stop=True)
            last.then_inc(s["setup_pe"], 1)
            pe.wait_ge(s["setup_dve"], 4)
            for half in range(2):
                for k, banks in ((2, (ps_q, ps_i)), (5, (ps_s, ps_c[0]))):
                    for b in range(4):
                        last = mm(banks[half][:, ts(b, D)], condT_b[:, 4 * half + b, :], wmod_sb[:, ts(k, D)],
                                  start=True, stop=True)
            last.then_inc(s["setup_pe"], 1)
            pe.wait_ge(w2_loaded, 128)
            nc.tensor.transpose(ps_c[1][:, 0:E], raw_r[:], ident[0:E, 0:E]).then_inc(s["setup_pe"], 1)
            pe.wait_ge(s["setup_act"], 4)
            pe.wait_ge(s["const_all"], 1)
            pe.wait_ge(s["dve_const"], 1)
            pe.wait_ge(s["setup_dve"], 11)

            def step(b, c):
                b3, c3, n = at(b, c, 3)

                def prefix(k):
                    if valid(n):
                        if k == 0:
                            pe.wait_ge(s["kv_done"], n + 1)
                        wait_count(pe, "qm_done", 3 * n - 2 + k)
                        h0, h1 = THIRDS[k]
                        w = HD * HV
                        mm(ps_c[k][:, 0:(h1 - h0) * w], tri[:], kv[:, c3 % 2, h0 * w:h1 * w],
                           start=True, stop=True).then_inc(s["C_done"], 1)

                prefix(0)
                b5, c5, m = at(b, c, 5)
                if valid(m):
                    pe.wait_ge(s["valT_done"], m + 1)
                    pe.wait_ge(s["woga_done"], b5 + 1)
                    wait_count(pe, "elu_done", m + 4, NCH)
                    wait_count(pe, "v_done", m + 4, NCH)
                    if not valid(m + 3):
                        pe.wait_ge(s["x1_done"], m)
                    mm(ps_a[:, 0:P], ones_b[:], gabo_parts[:, ts(b5, D)], start=True, stop=False)
                    mm(ps_a[:, 0:P], valT[:, c5 % 2, :], w_o_ga[:], start=False, stop=True).then_inc(s["y_done"], 1)
                prefix(1)
                _, c0, a = at(b, c, 0)
                if valid(a):
                    pe.wait_ge(s["xn_done"], a + 1)
                    wait_count(pe, "hT_done", a)
                    wait_count(pe, "h2T_done", a - 7)
                    wait_count(pe, "logits_done", a - 8)
                    nc.tensor.transpose(ps_t[:, 0:P], xn[:, c0 % 2, :], ident[:]).then_inc(s["xnT_done"], 1)
                prefix(2)
                if valid(n):
                    if c3 < CPB - 1:
                        wait_count(pe, "sbd_done", 7 * b3 + c3)
                        mm(ps_s[:, 0:FV], qk[:, c3 % 4, P:2 * P], v_aug[:, c3 % 4].rearrange("p h m -> p (h m)"),
                           start=(c3 == 0), stop=True, skip_group_check=True).then_inc(s["ktv_done"], 1)
                    if c3 > 0:
                        pe.wait_ge(s["qT_done"], n + 1)
                        pe.wait_ge(s["sbd_done"], 7 * b3 + c3)
                        wait_count(pe, "add_done", 7 * b3 + c3 - 1)
                        mm(ps_i[:, 0:FV], qT[:, c3 % 2, :], s_bd[:, (c3 - 1) % 2, :],
                           start=True, stop=True).then_inc(s["inter_done"], 1)
                _, c2, q = at(b, c, 2)
                if valid(q):
                    pe.wait_ge(s["elu_done"], q + 1)
                    wait_count(pe, "valT_done", q - 2)
                    wait_count(pe, "qT_done", q)
                    nc.tensor.transpose(ps_q[:, 0:P], qk[:, c2 % 4, 0:P], ident[:]).then_inc(s["qT_ps"], 1)
                _, c1, r = at(b, c, 1)
                if valid(r):
                    pe.wait_ge(s["hT_done"], r + 1)
                    wait_count(pe, "x1_done", r - 3)
                    wait_count(pe, "elu_done", r)
                    wait_count(pe, "v_done", r)
                    mm(ps_a[:, 0:3 * P], ones_b[:], bias_parts[:], start=True, stop=False)
                    mm(ps_a[:, 0:3 * P], hT[:, c1 % 2, :], w_qkv[:], start=False, stop=True)\
                        .then_inc(s["qkv_done"], 1)
                _, c4, v = at(b, c, 4)
                if valid(v):
                    pe.wait_ge(s["norm_done"], v + 1)
                    wait_count(pe, "qT_done", v + 3, NCH)
                    if not valid(v + 2):
                        pe.wait_ge(s["valT_done"], v)
                    nc.tensor.transpose(ps_q[:, 0:P], val[:, c4 % 2, :], ident[:]).then_inc(s["valT_ps"], 1)
                _, c8, l = at(b, c, 8)
                _, c7, u = at(b, c, 7)
                if valid(l):
                    pe.wait_ge(s["h2T_done"], l + 1)
                    wait_count(pe, "hT_done", l + 9, NCH)
                    wait_count(pe, "logits_done", l)
                    mm(ps_t[:, 256:256 + E], h2T_w[:, c8, :], rwT[:], start=True, stop=True)\
                        .then_inc(s["logits_ps"], 1)
                if valid(u):
                    pe.wait_ge(s["xn2_done"], u + 1)
                    wait_count(pe, "hT_done", u + 8, NCH)
                    wait_count(pe, "h2T_done", u)
                    nc.tensor.transpose(ps_t[:, 128:256], xn2[:, c7 % 2, :], ident[:]).then_inc(s["xn2T_ps"], 1)

            for c in range(CPB):
                step(0, c)
            with pe.Fori(1, B) as b:
                for c in range(CPB):
                    step(b, c)
            for c in range(CPB):
                step(B, c)

            pe.wait_ge(s["qm_done"], 3 * NCH)
            pe.wait_ge(s["x1_done"], NCH)
            pe.wait_ge(s["add_done"], 7 * B)
            pe.wait_ge(s["sbd_done"], 7 * B)
            pe.wait_ge(w2_loaded, 128)
            for bank_, shared, raw in ((ps_c[0], 0, raw_g), (ps_c[1], 1, raw_u), (ps_c[2], 2, raw_d)):
                for u in range(UNITS):
                    src = raw[:, u, :] if raw is not raw_d else raw_d[:, ts(u, P)]
                    dst = bank_[:, ts(u, P)] if u < 4 else ps_i[:, ts(shared, P)]
                    last = nc.tensor.transpose(dst, src, ident[:])
            last.then_inc(s["gate_pe"], 1)
            pe.wait_ge(s["gate_dve"], 21)
            mm(ps_a[:, 0:2 * E], ones_f[:], tot[:], start=True, stop=True).then_inc(s["gate_pe"], 1)
            def choice(b, first):
                pe.wait_ge(s["selw_done"], b + 1)
                if not first:
                    pe.wait_ge(s["selT_done"], b)
                sel_ps = ps_q[:].bitcast(BF16)
                for j in range(CPB):
                    last = nc.tensor.transpose(sel_ps[0:E, ts(j, P)], sel_w[:, ts(j, E)], ident_b[:])
                last.then_inc(s["selT_ps"], 1)

            choice(0, True)
            with pe.Fori(1, B) as b:
                choice(b, False)
            pe.wait_ge(s["selT_done"], B)
            pe.wait_ge(s["gate_dve"], 25)
            pe.wait_ge(s["gate_act"], 5)

            def gate_up(b, i):
                b, i = (b + 1, i - 10) if i >= 10 else (b, i)
                t, u = divmod(i, UNITS)
                m = b * 10 + i
                h2 = h2T_all[:, bass.ds(b * (CPB * P) + t * 512, 512)]
                wait_count(pe, "silu_done", m - 1)
                mm(ps_g[i % 2][:], gwT[:, u, :], h2, start=True, stop=(u == UNITS - 1))\
                    .then_inc(s["g_done"], 1)
                if u < UNITS - 1:
                    mm(ps_g[i % 2][:], pick[:, u].rearrange("e a i -> e (a i)"),
                       selT[:, bass.ds(b * (CPB * P) + t * 512, 512)], start=False, stop=True)\
                        .then_inc(s["g_done"], 1)
                wait_count(pe, "hid_done", m - 1)
                mm(ps_u[i % 2][:], uwT[:, u, :], h2, start=True, stop=True).then_inc(s["u_done"], 1)

            def down(b, i):
                t, u = divmod(i, UNITS)
                m = b * 10 + i
                pe.wait_ge(s["hid_done"], m + 1)
                if u == 0:
                    wait_count(pe, "ffn_done", 2 * b + t - 1)
                for j in range(4):
                    last = mm(ps_o[t][:, ts(j, P)], hid[:, i % 2, ts(j, P)], dwT[:, u, :],
                              start=(u == 0 and j == 0), stop=(u == UNITS - 1), skip_group_check=True)
                last.then_inc(s["down_done"], 1)

            def expert_row(b, last_row):
                for i in range(10):
                    if not (last_row and i == 9):
                        gate_up(b, i + 1)
                    down(b, i)

            for h in range(2):
                pe.wait_ge(h2T_stored[h], 16 * B)
            gate_up(0, 0)
            expert_row(0, False)
            with pe.Fori(1, B - 1) as b:
                expert_row(b, False)
            expert_row(B - 1, True)

        @block.scalar
        def _(act):
            A = nc.scalar.activation
            act.wait_ge(s["setup_pe"], 1)
            act.wait_ge(s["dve_const"], 1)
            A(lnv[:, 0:1], neg1[:], ACT.Ln, scale=-1.0).then_inc(s["setup_act"], 1)
            A(condT[:, 0, :], ps_t[:, 0:B], ACT.Exp, scale=-1.0).then_inc(s["setup_act"], 1)
            act.wait_ge(s["setup_pe"], 2)
            A(modT[:].rearrange("p k b -> p (k b)"), ps_a[:, 0:6 * B], ACT.Copy).then_inc(s["setup_act"], 1)
            act.wait_ge(s["setup_pe"], 4)
            A(rwT[:], ps_c[1][:, 0:E], ACT.Copy)
            A(ga_bc[:, 0:512], ps_q[:], ACT.Copy)
            A(ga_bc[:, 512:1024], ps_i[:], ACT.Copy)
            A(gb_bc[:, 0:512], ps_s[:], ACT.Copy)
            A(gb_bc[:, 512:1024], ps_c[0][:], ACT.Copy).then_inc(s["setup_act"], 1)
            act.wait_ge(s["setup_dve"], 5)

            def norm_act(n_pair, lo, hi):
                act.wait_ge(s["ve_done"], n_pair + 1)
                A(lnv[:, lo:hi], ve[:, lo:hi], ACT.Ln).then_inc(s["rs_act"], 1)
                act.wait_ge(s["rs_act"], 2 * n_pair + 1)
                A(y0[:, lo:hi], lnv[:, lo:hi], ACT.Exp, scale=-0.5).then_inc(s["rs_act"], 1)

            def xn1(b, c):
                a_b, a_c, a = b, c, b * CPB + c
                if c == CPB:
                    a_b, a_c, a = b + 1, 0, (b + 1) * CPB
                if isinstance(a, int) and a >= NCH:
                    return
                pair = b * 4 + c // 2
                act.wait_ge(s["ln_done"], pair + 1)
                wait_count(act, "xnT_done", a - 1)
                par, col = (c // 2) % 2, c % 2
                A(xn[:, a_c % 2, :], x_all[:, ts(a, P)], ACT.Identity, bias=nmr[:, par, col:col + 1],
                  scale=rstd[:, par, col:col + 1]).then_inc(s["xn_done"], 1)

            def step(b, c):
                _, c0, a = at(b, c, 0)
                if valid(a):
                    if c == 0:
                        A(mod1[:], modT[:, 0:2, bass.ds(b, 1)].rearrange("p k o -> p (k o)"), ACT.Copy)\
                            .then_inc(s["mod1_done"], 1)
                        act.wait_ge(s["mod1_done"], b + 1)
                    act.wait_ge(s["xnT_done"], a + 1)
                    wait_count(act, "qkv_done", a - 1)
                    A(hT[:, c0 % 2, :], ps_t[:, 0:P], ACT.Identity, bias=mod1[:, 0:1],
                      scale=mod1[:, 1:2]).then_inc(s["hT_done"], 1)
                _, c7, u = at(b, c, 7)
                if valid(u):
                    j = c7 % 2
                    pair = b * 4 + (c - 1) // 2 + 1 if c else b * 4
                    act.wait_ge(s["ln_done"], pair + 1)
                    wait_count(act, "xn2T_ps", u - 1)
                    par = pair_par(c)
                    A(xn2[:, j, :], x_all[:, ts(u, P)], ACT.Identity, bias=nmr[:, par, 2 + j:3 + j],
                      scale=rstd[:, par, 2 + j:3 + j]).then_inc(s["xn2_done"], 1)
                _, c2, q = at(b, c, 2)
                b2 = b - 1 if c < 2 else b
                if valid(q):
                    act.wait_ge(s["qT_ps"], q + 1)
                    bq_, cq_, _ = at(b, c, 4)
                    wait_count(act, "inter_done", 7 * bq_ + cq_)
                    A(qT[:, c2 % 2, :], ps_q[:, 0:P], ACT.Copy).then_inc(s["qT_done"], 1)
                _, c1, r = at(b, c, 1)
                if valid(r):
                    act.wait_ge(s["qkv_done"], r + 1)
                    bk_, ck_, old = at(b, c, 5)
                    wait_count(act, "ktv_done", 7 * bk_ + min(ck_ + 1, 7))
                    wait_count(act, "kv_done", r - 3)
                    A(v_aug[:, c1 % 4, :, 0:HD], ps_a[:, 2 * P:3 * P].rearrange("p (h m) -> p h m", m=HD),
                      ACT.Copy).then_inc(s["v_done"], 1)
                    wait_count(act, "elu_done", r - 1)
                    A(e_qk[:, c1 % 2, :], ps_a[:, 0:2 * P], ACT.Exp, bias=neg1[:]).then_inc(s["exp_done"], 1)
                _, c4, v = at(b, c, 4)
                if valid(v):
                    act.wait_ge(s["valT_ps"], v + 1)
                    wait_count(act, "y_done", v - 1)
                    A(valT[:, c4 % 2, :], ps_q[:, 0:P], ACT.Copy).then_inc(s["valT_done"], 1)
                _, c8, l = at(b, c, 8)
                if valid(l):
                    act.wait_ge(s["logits_ps"], l + 1)
                    if valid(u):
                        act.wait_ge(s["xn2T_ps"], u + 1)
                    A(logits[:, ts(l, E)], ps_t[:, 256:256 + E], ACT.Copy).then_inc(s["logits_done"], 1)
                if valid(u):
                    b7, _, _ = at(b, c, 7)
                    if c7 == 0:
                        A(mod2[:], modT[:, 3:5, bass.ds(b7, 1)].rearrange("p k o -> p (k o)"), ACT.Copy)\
                            .then_inc(s["mod2_done"], 1)
                        act.wait_ge(s["mod2_done"], b7 + 1)
                    act.wait_ge(s["xn2T_ps"], u + 1)
                    if not isinstance(b7, int) or b7 > 0:
                        act.wait_ge(h2T_stored[c7 // 4], b7 * 16)
                    A(h2T_w[:, c7, :], ps_t[:, 128:256], ACT.Identity, bias=mod2[:, 0:1],
                      scale=mod2[:, 1:2]).then_inc(s["h2T_done"], 1)
                if c % 2 == 0 and (not isinstance(b, int) or b * CPB + c <= NCH + 4):
                    lo, hi = pair_cols(b, c)
                    norm_act(b * 4 + c // 2 + 1, lo, hi)
                xn1(b, c + 1)

            norm_act(0, 0, 2)
            xn1(0, 0)
            for c in range(CPB):
                step(0, c)
            with act.Fori(1, B) as b:
                for c in range(CPB):
                    step(b, c)
            for c in range(CPB):
                step(B, c)

            act.wait_ge(s["gate_pe"], 1)
            A(gwT[:, 0:4, :].rearrange("p u d -> p (u d)"), ps_c[0][:], ACT.Copy).then_inc(s["gate_act"], 1)
            A(uwT[:, 0:4, :].rearrange("p u d -> p (u d)"), ps_c[1][:], ACT.Copy).then_inc(s["gate_act"], 1)
            A(dwT[:, 4, :], ps_i[:, 256:384], ACT.Copy)
            A(gwT[:, 4, :], ps_i[:, 0:128], ACT.Copy)
            A(uwT[:, 4, :], ps_i[:, 128:256], ACT.Copy).then_inc(s["gate_act"], 1)
            act.wait_ge(s["gate_dve"], 1)
            A(gl[1][:], gl[0][:], ACT.Exp, scale=-1.0).then_inc(s["gate_act"], 1)

            A(dwT[:, 0:4, :].rearrange("p u d -> p (u d)"), ps_c[2][:], ACT.Copy).then_inc(s["gate_act"], 1)

            def choice(b):
                act.wait_ge(s["selT_ps"], b + 1)
                A(selT[:, ts(b, CPB * P)], ps_q[0:E, :].bitcast(BF16), ACT.Copy).then_inc(s["selT_done"], 1)

            with act.Fori(0, B) as b:
                choice(b)

            def expert_row(b):
                for i in range(10):
                    m = b * 10 + i
                    masks = i + 1 - (i + 1) // UNITS
                    act.wait_ge(s["g_done"], b * 18 + i + 1 + masks)
                    wait_count(act, "hid_done", m - 1)
                    A(silu_g[:, i % 2, :], ps_g[i % 2][:], ACT.Silu).then_inc(s["silu_done"], 1)

            expert_row(0)
            with act.Fori(1, B) as b:
                expert_row(b)

        @block.vector
        def _(dve):
            V = nc.vector
            V.memset(neg1[:], -1.0)
            V.memset(ones_b[:], 1.0)
            V.memset(v_aug[:], 1.0)
            V.memset(bias_parts[:], 0.0)
            V.memset(gabo_parts[:], 0.0).then_inc(s["dve_const"], 1)
            dve.wait_ge(s["setup_act"], 2)
            V.tensor_scalar(condT[:, 0, :], condT[:, 0, :], 1.0, None, ALU.add).then_inc(s["setup_dve"], 1)
            dve.wait_ge(s["setup_dve"], 1)
            V.reciprocal(condT[:, 1, :], condT[:, 0, :]).then_inc(s["setup_dve"], 1)
            dve.wait_ge(s["setup_dve"], 2)
            V.tensor_tensor(condT[:, 2, :], ps_t[:, 0:B], condT[:, 1, :], ALU.mult).then_inc(s["setup_dve"], 1)
            dve.wait_ge(s["setup_dve"], 3)
            V.tensor_copy(condT_b[:], condT[:, 2, :].rearrange("p (b o) -> p b o", o=1).broadcast_to([P, B, P]))\
                .then_inc(s["setup_dve"], 1)
            dve.wait_ge(s["setup_act"], 3)
            V.tensor_scalar(modT[:, 1, :], modT[:, 1, :], 1.0, None, ALU.add)
            V.tensor_scalar(modT[:, 4, :], modT[:, 4, :], 1.0, None, ALU.add)\
                .then_inc(s["setup_dve"], 1)
            V.tensor_scalar(bias_row[0:1, 0:2 * P], bias_row[0:1, 0:2 * P], 1.0, None, ALU.add)\
                .then_inc(s["setup_dve"], 1)
            dve.wait_ge(s["setup_dve"], 6)
            split_row(dve, bias_parts, bias_row, 3 * P, s["setup_dve"], 6)
            dve.wait_ge(s["setup_act"], 4)
            k = 11
            for g in (ga_bc, gb_bc):
                V.tensor_scalar(sgn_bc[:], g[:], 0.0, 2.0, ALU.is_ge, ALU.mult).then_inc(s["setup_dve"], 1)
                k += 1
                dve.wait_ge(s["setup_dve"], k)
                V.tensor_scalar(sgn_bc[:], sgn_bc[:], -1.0, None, ALU.add).then_inc(s["setup_dve"], 1)
                k += 1
                dve.wait_ge(s["setup_dve"], k)
                V.tensor_tensor(g[:], g[:], sgn_bc[:], ALU.mult).then_inc(s["setup_dve"], 1)
                k += 1
                dve.wait_ge(s["setup_dve"], k)
                V.scalar_tensor_tensor(out=g[:], in0=g[:], scalar=0.25, in1=sgn_bc[:], op0=ALU.max, op1=ALU.mult)\
                    .then_inc(s["setup_dve"], 1)
                k += 1
                dve.wait_ge(s["setup_dve"], k)
            V.tensor_tensor(gabo_row[0:1, :].rearrange("p (b d) -> p b d", d=D),
                            ga_bc[0:1, :].rearrange("p (b d) -> p b d", d=D),
                            bo_row[0:1, :].rearrange("p (b d) -> p b d", b=1).broadcast_to([1, B, D]),
                            ALU.mult).then_inc(s["setup_dve"], 1)
            k += 1
            dve.wait_ge(s["setup_dve"], k)
            split_row(dve, gabo_parts, gabo_row, B * D, s["setup_dve"], k)
            V.tensor_tensor(w_o_ga[:], w_o[:], ga_bc[:, 0:D], ALU.mult).then_inc(s["woga_done"], 1)

            def statistics(lo, hi, chunks):
                for col in range(lo, hi):
                    V.bn_stats(st[:, col, :], x_all[:, ts(chunks[col], P)]).then_inc(s["stat_done"], 1)

            def mean_var(lo, hi, before):
                for col in range(lo, hi):
                    V.bn_aggr(agg[:, col, :], st[:, col, :]).then_inc(s["agg_done"], 1)
                dve.wait_ge(s["agg_done"], before + hi - lo)
                V.tensor_scalar(ve[:, lo:hi], agg[:, lo:hi, 1], LN_EPS, None, ALU.add).then_inc(s["ve_done"], 1)

            def newton(pair, par, lo, hi):
                dve.wait_ge(s["rs_act"], 2 * pair + 2)
                V.tensor_tensor(nt1[:, lo:hi], y0[:, lo:hi], y0[:, lo:hi], ALU.mult).then_inc(s["newton"], 1)
                dve.wait_ge(s["newton"], 4 * pair + 1)
                V.tensor_tensor(nt2[:, lo:hi], nt1[:, lo:hi], ve[:, lo:hi], ALU.mult).then_inc(s["newton"], 1)
                dve.wait_ge(s["newton"], 4 * pair + 2)
                V.tensor_scalar(nt1[:, lo:hi], nt2[:, lo:hi], -0.5, 1.5, ALU.mult, ALU.add).then_inc(s["newton"], 1)
                dve.wait_ge(s["newton"], 4 * pair + 3)
                wait_count(dve, "xn_done", 2 * pair - 2, NCH)
                wait_count(dve, "xn2_done", 2 * pair - 10)
                V.tensor_tensor(rstd[:, par, lo:hi], y0[:, lo:hi], nt1[:, lo:hi], ALU.mult).then_inc(s["newton"], 1)
                dve.wait_ge(s["newton"], 4 * pair + 4)
                V.scalar_tensor_tensor(out=nmr[:, par, lo:hi], in0=agg[:, lo:hi, 0], scalar=-1.0,
                                       in1=rstd[:, par, lo:hi], op0=ALU.mult, op1=ALU.mult)\
                    .then_inc(s["ln_done"], 1)

            def step(b, c):
                is_reg = not isinstance(b, int)
                no = b * CPB + c
                b3, c3, n = at(b, c, 3)
                if valid(n):
                    q = qk[:, c3 % 4, 0:P]
                    wait_count(dve, "red_done", n)
                    for k, (h0, h1) in enumerate(THIRDS):
                        dve.wait_ge(s["C_done"], 3 * n + k + 1)
                        rows = (h1 - h0) * HD
                        V.tensor_tensor(prod[:, h0 * HD * HV:h1 * HD * HV].rearrange("p (r m) -> p r m", m=HV),
                                        ps_c[k][:, 0:rows * HV].rearrange("p (r m) -> p r m", m=HV),
                                        q[:, h0 * HD:h1 * HD].rearrange("p (r o) -> p r o", o=1)
                                        .broadcast_to([P, rows, HV]), ALU.mult).then_inc(s["qm_done"], 1)
                b5, c5, m = at(b, c, 5)
                if valid(m):
                    dve.wait_ge(s["y_done"], m + 1)
                    V.tensor_tensor(x_all[:, ts(m, P)], ps_a[:, 0:P], x_all[:, ts(m, P)], ALU.add)\
                        .then_inc(s["x1_done"], 1)
                    if c5 == CPB - 1 and (is_reg or b < B):
                        V.tensor_tensor(w_o_ga[:], w_o[:], ga_bc[:, ts(b, D)], ALU.mult).then_inc(s["woga_done"], 1)
                pairs = c % 2 == 0 and (is_reg or no <= NCH + 4)
                if pairs:
                    lo, hi = pair_cols(b, c)
                    if hi == 4:
                        dve.wait_ge(s["x1_done"], no - 4)
                    pair = b * 4 + c // 2 + 1
                    statistics(lo, hi, [no + 2, no + 3, no - 6, no - 5])
                    dve.wait_ge(s["stat_done"], stat_before(pair) + hi - lo)
                if valid(n):
                    dve.wait_ge(s["qm_done"], 3 * n + 3)
                    V.tensor_reduce(red[:].rearrange("p (h m) -> p h m", m=HV),
                                    prod[:].rearrange("p (h d m) -> p h m d", d=HD, m=HV), AX_X, ALU.add)\
                        .then_inc(s["red_done"], 1)
                if pairs:
                    mean_var(lo, hi, stat_before(pair))
                _, c1, r = at(b, c, 1)
                if valid(r):
                    dve.wait_ge(s["exp_done"], r + 1)
                    bo_, co_, old = at(b, c, 5)
                    wait_count(dve, "kv_done", r - 3)
                    wait_count(dve, "ktv_done", 7 * bo_ + min(co_ + 1, 7))
                    wait_count(dve, "qT_ps", r - 3)
                    V.scalar_tensor_tensor(out=qk[:, c1 % 4, :], in0=e_qk[:, c1 % 2, :], scalar=1.0,
                                           in1=ps_a[:, 0:2 * P], op0=ALU.min, op1=ALU.max).then_inc(s["elu_done"], 1)
                if valid(n):
                    src = red
                    dve.wait_ge(s["red_done"], n + 1)
                    if c3 > 0:
                        dve.wait_ge(s["inter_done"], 7 * b3 + c3)
                        V.tensor_tensor(nd[:], ps_i[:, 0:FV], red[:], ALU.add).then_inc(s["add_done"], 1)
                        src = nd
                    if c3 < CPB - 1:
                        dve.wait_ge(s["ktv_done"], 7 * b3 + c3 + 1)
                        V.tensor_tensor(s_bd[:, c3 % 2, :], ps_s[:, 0:FV], head_mask[:], ALU.mult)\
                            .then_inc(s["sbd_done"], 1)
                    if c3 > 0:
                        dve.wait_ge(s["add_done"], 7 * b3 + c3)
                    num = src[:].rearrange("p (h m) -> p h m", m=HV)
                    V.tensor_scalar(den[:], num[:, :, HD], 1e-6, None, ALU.add).then_inc(s["den_done"], 1)
                    dve.wait_ge(s["den_done"], n + 1)
                    V.reciprocal(rec[:], den[:]).then_inc(s["rec_done"], 1)
                    dve.wait_ge(s["rec_done"], n + 1)
                    wait_count(dve, "valT_ps", n - 1)
                    V.tensor_tensor(val[:, c3 % 2, :].rearrange("p (h m) -> p h m", m=HD), num[:, :, 0:HD],
                                    rec[:].rearrange("p (h o) -> p h o", o=1).broadcast_to([P, HEADS, HD]),
                                    ALU.mult).then_inc(s["norm_done"], 1)
                if pairs:
                    newton(pair, (c // 2 + 1) % 2, lo, hi)

            dve.wait_ge(x_loaded[0], 16)
            dve.wait_ge(s["const_all"], 1)
            statistics(0, 2, [0, 1])
            dve.wait_ge(s["stat_done"], 2)
            mean_var(0, 2, 0)
            newton(0, 0, 0, 2)
            for c in range(CPB):
                if c == 6:
                    dve.wait_ge(x_loaded[1], 16)
                step(0, c)
            for b in range(2, B):
                dve.wait_ge(x_loaded[b], 16)
            with dve.Fori(1, B) as b:
                for c in range(CPB):
                    step(b, c)
            for c in range(CPB):
                step(B, c)

            n = [0]

            def link(ins):
                ins.then_inc(s["gate_dve"], 1)
                n[0] += 1
                dve.wait_ge(s["gate_dve"], n[0])

            def by_chunk(t):
                return t.rearrange("p (n e) -> p n e", e=E)

            def over_e(t):
                return t.rearrange("p (n o) -> p n o", o=1).broadcast_to([P, NCH, E])

            row = [P, NCH, E]
            order_b = order[:].rearrange("p (o e) -> p o e", o=1).broadcast_to(row)
            dve.wait_ge(s["logits_done"], NCH)
            link(V.tensor_tensor(by_chunk(gl[0][:]), by_chunk(logits[:]),
                                 lb_bc[:].rearrange("p (o e) -> p o e", o=1).broadcast_to(row), ALU.add))
            dve.wait_ge(s["gate_act"], 4)
            link(V.tensor_scalar(gl[1][:], gl[1][:], 1.0, None, ALU.add))
            link(V.reciprocal(gl[0][:], gl[1][:]))
            for k in range(2):
                best, mk, one = gm[:, k, :], gm[:, 2 + k, :], gl[2 + k]
                link(V.tensor_reduce(best, by_chunk(gl[0][:]), AX_X, ALU.max))
                link(V.tensor_tensor(by_chunk(gl[4][:]), by_chunk(gl[0][:]), over_e(best), ALU.is_equal))
                link(V.tensor_tensor(by_chunk(gl[4][:]), by_chunk(gl[4][:]), order_b, ALU.mult))
                link(V.tensor_reduce(mk, by_chunk(gl[4][:]), AX_X, ALU.max))
                link(V.tensor_tensor(by_chunk(one[:]), by_chunk(gl[4][:]), over_e(mk), ALU.is_equal))
                if k == 0:
                    link(V.scalar_tensor_tensor(out=gl[0][:], in0=one[:], scalar=-4.0, in1=gl[0][:],
                                                op0=ALU.mult, op1=ALU.add))
            link(V.scalar_tensor_tensor(out=gm[:, 4, :], in0=gm[:, 0, :], scalar=1e-8, in1=gm[:, 1, :],
                                        op0=ALU.add, op1=ALU.add))
            link(V.reciprocal(gm[:, 5, :], gm[:, 4, :]))
            link(V.tensor_tensor(gm[:, 0:2, :], gm[:, 0:2, :],
                                 gm[:, 5:6, :].broadcast_to([P, 2, NCH]), ALU.mult))
            link(V.tensor_tensor(by_chunk(gl[4][:]), by_chunk(gl[2][:]), over_e(gm[:, 0, :]), ALU.mult))
            link(V.tensor_tensor(by_chunk(gl[5][:]), by_chunk(gl[3][:]), over_e(gm[:, 1, :]), ALU.mult))
            V.tensor_tensor(gl[2][:], gl[2][:], gl[3][:], ALU.add)
            link(V.tensor_tensor(gl[4][:], gl[4][:], gl[5][:], ALU.add))
            V.tensor_scalar(sel_m1[:], gl[2][:], -1.0, None, ALU.add)
            V.tensor_reduce(tot[:, 0:E], gl[4][:].rearrange("p (n e) -> p e n", e=E), AX_X, ALU.add)
            link(V.tensor_reduce(tot[:, E:2 * E], gl[2][:].rearrange("p (n e) -> p e n", e=E), AX_X, ALU.add))
            def choice(b):
                wait_count(dve, "selT_ps", b)
                V.tensor_copy(sel_w[:], sel_m1[:, ts(b, CPB * E)]).then_inc(s["selw_done"], 1)

            choice(0)
            dve.wait_ge(s["gate_pe"], 2)
            link(V.tensor_scalar(wmean[:, 0, :], ps_a[:, E:2 * E], 1.0, None, ALU.max))
            link(V.reciprocal(wmean[:, 1, :], wmean[:, 0, :]))
            link(V.tensor_tensor(wmean[:, 2, :], ps_a[:, 0:E], wmean[:, 1, :], ALU.mult))
            dve.wait_ge(s["gate_act"], 5)
            for u in range(UNITS - 1):
                for a in range(2):
                    rows = slice(a * I, (a + 1) * I)
                    last = V.tensor_scalar(dwT[rows, u, :], dwT[rows, u, :], wmean[rows, 2, 2 * u + a:2 * u + a + 1],
                                           None, ALU.mult)
            link(last)
            with dve.Fori(1, B) as b:
                choice(b)

            def finish(tile, b, t):
                dve.wait_ge(s["down_done"], UNITS * (tile + 1))
                wait_count(dve, "fin_done", tile)
                V.tensor_tensor(ffn[:].rearrange("p (j d) -> p j d", d=D),
                                ps_o[t][:].rearrange("p (j d) -> p j d", d=D),
                                gb_bc[:, ts(b, D)].rearrange("p (o d) -> p o d", o=1).broadcast_to([P, 4, D]),
                                ALU.mult).then_inc(s["ffn_done"], 1)
                dve.wait_ge(s["ffn_done"], tile + 1)
                xs = x_all[:, bass.ds(b * (CPB * P) + t * 512, 512)]
                V.tensor_tensor(xs, xs, ffn[:], ALU.add).then_inc(s["fin_done"], 1)

            def expert_row(b):
                for i in range(10):
                    m = b * 10 + i
                    dve.wait_ge(s["silu_done"], m + 1)
                    dve.wait_ge(s["u_done"], m + 1)
                    wait_count(dve, "down_done", m - 1)
                    V.tensor_tensor(hid[:, i % 2, :], silu_g[:, i % 2, :], ps_u[i % 2][:], ALU.mult)\
                        .then_inc(s["hid_done"], 1)
                    if i == 1 and (not isinstance(b, int) or b > 0):
                        finish(2 * b - 1, b - 1, 1)
                    if i == 6:
                        finish(2 * b, b, 0)

            expert_row(0)
            with dve.Fori(1, B) as b:
                expert_row(b)
            finish(TILES - 1, B - 1, 1)


_INS = ['L0_attn_x', 'L0_attn_Wq', 'L0_attn_bq', 'L0_attn_Wk', 'L0_attn_bk', 'L0_attn_Wv', 'L0_attn_bv',
        'L0_attn_Wo', 'L0_attn_bo', 'L0_ffn_gate_w', 'L0_ffn_lb_bias', 'L0_ffn_expert_gate_w',
        'L0_ffn_expert_up_w', 'L0_ffn_expert_down_w', 'L0_ffn_shared_gate_w', 'L0_ffn_shared_up_w',
        'L0_ffn_shared_down_w', 'L0_c', 'L0_wmod']
_OUTS = [((8, 1024, 128), 'float32')]


def kernel(**inputs):
    import numpy as _np
    import concourse.bacc as _bacc
    from concourse import mybir as _mybir
    from concourse.bass_utils import run_bass_kernel_spmd as _run

    nc = _bacc.Bacc("TRN2", target_bir_lowering=False, num_devices=1)
    arrays, args = {}, []
    for name in _INS:
        a = _np.ascontiguousarray(inputs[name])
        arrays[f"in_{name}_dram"] = a
        args.append(nc.dram_tensor(f"in_{name}_dram", a.shape, _mybir.dt.from_np(a.dtype), kind="ExternalInput").ap())
    for i, (shape, dtype) in enumerate(_OUTS):
        dt = _mybir.dt.from_np(_np.dtype(dtype))
        args.append(nc.dram_tensor(f"out_{i}_dram", shape, dt, kind="ExternalOutput").ap())
    adaln_block(nc, *args)
    r = _run(nc, [arrays], core_ids=[0])
    got = tuple(r.results[0][f"out_{i}_dram"] for i in range(len(_OUTS)))
    return got[0]
```

```python
from contextlib import ExitStack

import concourse.bass as bass
from concourse import mybir

F32 = mybir.dt.float32
BF16 = mybir.dt.bfloat16
ALU = mybir.AluOpType
ACT = mybir.ActivationFunctionType
AX_X = mybir.AxisListType.X
ts = bass.ts

P = 128
CPB = 8
HEADS, HD = 16, 8
HV = HD + 1
FV = HEADS * HV
KVW = HEADS * HD * HV
THIRDS = [(0, 6), (6, 11), (11, 16)]
UNITS = 5
MASKED_OUT = -1.0e30
LN_EPS = 1e-5


def at(b, c, lag):
    while lag > c:
        b, c = b - 1, c + CPB
    return b, c - lag, b * CPB + (c - lag)


def adaln_block(nc, x_in, wq, bq, wk, bk, wv, bv, wo, bo, gate_w, lb_bias, eg_w, eu_w, ed_w,
                sg_w, su_w, sd_w, cond, wmod, out):
    B, S, D = x_in.shape
    E, I, _ = eg_w.shape
    NCH = B * S // P
    assert D == P and S == CPB * P and E * I == (UNITS - 1) * P and D == HEADS * HD
    XCH = NCH + 2
    TILES = B * 2

    with ExitStack() as ctx:
        def sb(name, shape, dt=F32):
            return ctx.enter_context(nc.sbuf_tensor(name, shape, dt))

        def bank(name):
            return ctx.enter_context(nc.psum_tensor(name, [P, 512], F32))

        def sem(name):
            return ctx.enter_context(nc.semaphore(name))

        x_all = sb("x_all", [P, XCH * P])
        h2T_all = sb("h2T_all", [P, NCH * P])
        w_qkv = sb("w_qkv", [P, 3 * P])
        w_o = sb("w_o", [P, P])
        w_o_ga = sb("w_o_ga", [P, P])
        wmod_sb = sb("wmod_sb", [P, 6 * D])
        cond_sb = sb("cond_sb", [B, D])
        condT = sb("condT", [P, 3, B])
        spread = sb("spread", [B, B, P])
        modT = sb("modT", [P, 6, B])
        mod1 = sb("mod1", [P, 2])
        mod2 = sb("mod2", [P, 2])
        ga_bc = sb("ga_bc", [P, B * D])
        gb_bc = sb("gb_bc", [P, B * D])
        g_raw = sb("g_raw", [B, 2 * D])
        g_sgn = sb("g_sgn", [B, 2 * D])
        g8 = sb("g8", [B, 2 * D])
        lb_bc = sb("lb_bc", [P, E])
        raw_g = sb("raw_g", [P, UNITS, D])
        raw_u = sb("raw_u", [P, UNITS, D])
        raw_d = sb("raw_d", [P, UNITS * P])
        raw_r = sb("raw_r", [E, D])
        gwT = sb("gwT", [P, UNITS, P])
        uwT = sb("uwT", [P, UNITS, P])
        dwT = sb("dwT", [P, UNITS, P])
        rwT = sb("rwT", [P, E])
        ident = sb("ident", [P, P])
        ident_b = sb("ident_b", [P, P], BF16)
        tri = sb("tri", [P, P])
        head_mask = sb("head_mask", [P, FV])
        pick = sb("pick", [E, UNITS - 1, 2, I], BF16)
        ones_b = sb("ones_b", [P, P], BF16)
        ones_f = sb("ones_f", [P, P])
        neg1 = sb("neg1", [P, 1])
        order = sb("order", [P, E])
        bias_row = sb("bias_row", [1, 3 * P])
        bo_8 = sb("bo_8", [B, P])
        rest = sb("rest", [B, 3 * P])
        bias_parts = sb("bias_parts", [P, 3 * P], BF16)
        gabo = sb("gabo", [B, D])
        gabo_p = sb("gabo_p", [B, 3, D], BF16)
        gabo_parts = sb("gabo_parts", [P, B * D], BF16)

        st = sb("st", [P, 4, 6])
        agg = sb("agg", [P, 2, 4, 2])
        half_m = sb("half_m", [P, 4])
        minus_1 = sb("minus_1", [P, 4])
        eps = sb("eps", [P, 4])
        ve = sb("ve", [P, 4])
        neg_mean = sb("neg_mean", [P, 4])
        rstd = sb("rstd", [P, 2, 4])
        nmr = sb("nmr", [P, 2, 4])
        xn = sb("xn", [P, 2, P])
        xn2 = sb("xn2", [P, 2, P])
        hT = sb("hT", [P, 2, P])
        h2T_w = sb("h2T_w", [P, CPB, P])
        e_qk = sb("e_qk", [P, 2, 2 * P])
        qk = sb("qk", [P, 4, 2 * P])
        v_aug = sb("v_aug", [P, 4, HEADS, HV])
        kv = sb("kv", [P, 2, KVW])
        qT = sb("qT", [P, 2, P])
        s_full = sb("s_full", [P, FV])
        s_bd = sb("s_bd", [P, 2, FV])
        prod = sb("prod", [P, KVW])
        red = sb("red", [P, FV])
        nd = sb("nd", [P, FV])
        den = sb("den", [P, HEADS])
        rec = sb("rec", [P, HEADS])
        val = sb("val", [P, 2, P])
        valT = sb("valT", [P, 2, P])

        logits = sb("logits", [P, NCH * E])
        gl = [sb(f"gl{i}", [P, NCH * E]) for i in range(6)]
        gm = sb("gm", [P, 6, NCH])
        sel_m1 = sb("sel_m1", [P, NCH * E], BF16)
        sel_w = sb("sel_w", [P, CPB * E], BF16)
        selT = sb("selT", [E, NCH * P], BF16)
        tot = sb("tot", [P, 2 * E])
        wmean = sb("wmean", [P, 3, E])
        silu_g = sb("silu_g", [P, 2, 512])
        hid = sb("hid", [P, 2, 512])
        ffn = sb("ffn", [P, 512])

        ps_t = bank("ps_t")
        ps_a = bank("ps_a")
        ps_q = bank("ps_q")
        ps_i = bank("ps_i")
        ps_s = bank("ps_s")
        ps_c = [bank(f"ps_c{k}") for k in range(3)]
        ps_g = [ps_t, ps_a]
        ps_u = [ps_q, ps_i]
        ps_o = [ps_s, ps_c[0]]

        x_loaded = [sem(f"x_loaded{b}") for b in range(B)]
        w_loaded = sem("w_loaded")
        w2_loaded = sem("w2_loaded")
        out_stored = sem("out_stored")
        names = """const_ident const_all dve_const gabo_split setup_pe setup_act setup_dve
            xn_done xnT_done hT_done qkv_done v_done exp_done elu_done kv_done C_done qm_done red_done
            qT_ps qT_done ktv_done s_read sbd_done inter_done add_done den_done rec_done norm_done
            valT_ps valT_done y_done x1_done woga_done stat_done agg_done ve_done rstd_done ln_done
            mod1_done mod2_done xn2_done xn2T_ps h2T_done logits_ps logits_done
            gb_ps gb_done gate_dve gate_act gate_pe selw_done selT_ps selT_done
            g_done u_done silu_done hid_done down_done ffn_done fin_done""".split()
        s = {n: sem(n) for n in names}
        gabo_moved = sem("gabo_moved")
        h2T_stored = [sem("h2T_stored0"), sem("h2T_stored1")]

        def split_row(dve, part, row, rows, n, done, base):
            for k in range(3):
                src = row if k == 0 else rest
                nc.vector.tensor_copy(part(k), src[0:rows, 0:n]).then_inc(done, 1)
                dve.wait_ge(done, base + 2 * k + 1)
                if k < 2:
                    nc.vector.tensor_copy(hop[0:rows, 0:n], part(k)).then_inc(done, 1)
                    dve.wait_ge(done, base + 2 * k + 2)
                    nc.vector.tensor_tensor(rest[0:rows, 0:n], src[0:rows, 0:n], hop[0:rows, 0:n],
                                            ALU.subtract).then_inc(s["rest_done"], 1)
                    rest_count[0] += 1
                    dve.wait_ge(s["rest_done"], rest_count[0])

        s["rest_done"] = sem("rest_done")
        rest_count = [0]
        hop = sb("hop", [B, 3 * P])

        block = ctx.enter_context(nc.Block())

        def pair_par(c):
            return ((c - 1) // 2 + 1) % 2 if c else 0

        def pair_cols(b, c):
            if isinstance(b, int):
                step_no = b * CPB + c
                return (0 if step_no + 2 < NCH else 2), (4 if step_no >= 6 else 2)
            return 0, 4

        def stat_before(pair):
            if isinstance(pair, int):
                return sum(2 if p < 4 or p > NCH // 2 else 4 for p in range(pair))
            return 4 * pair - 8

        def valid(n):
            return not isinstance(n, int) or 0 <= n < NCH

        def wait_count(eng, name, value, cap=None):
            if isinstance(value, int):
                if cap is not None:
                    value = min(value, cap)
                if value <= 0:
                    return
            eng.wait_ge(s[name], value)

        @block.sync
        def _(sp):
            def load(dst, src, done):
                sp.dma_start(dst, src).then_inc(done, 16)

            x_rows = x_in.rearrange("b (c p) d -> b p c d", p=P)
            out_rows = out.rearrange("b (t c p) d -> b t p c d", p=P, c=4)

            def x_batch(b):
                return x_all[:, ts(b, CPB * P)].rearrange("p (c d) -> p c d", d=D)

            load(x_batch(0), x_rows[0], x_loaded[0])
            load(cond_sb[:], cond, w_loaded)
            load(wmod_sb[:], wmod, w_loaded)
            for k, (w, b_) in enumerate(((wq, bq), (wk, bk), (wv, bv))):
                load(w_qkv[:, ts(k, P)], w, w_loaded)
                load(bias_row[0:1, ts(k, P)], b_.rearrange("(a n) -> a n", a=1), w_loaded)
            load(w_o[:], wo, w_loaded)
            load(bo_8[:], bo.rearrange("(a n) -> a n", a=1).to_broadcast([B, P]), w_loaded)
            load(raw_r[:], gate_w, w2_loaded)
            load(lb_bc[:], lb_bias.rearrange("(a n) -> a n", a=1).to_broadcast([P, E]), w2_loaded)
            for raw, we, ws in ((raw_g, eg_w, sg_w), (raw_u, eu_w, su_w)):
                load(raw[:, 0:UNITS - 1, :], we.rearrange("e i d -> (e i) d").rearrange("(u p) d -> p u d", p=P),
                     w2_loaded)
                load(raw[:, UNITS - 1, :], ws, w2_loaded)
            load(raw_d[:, 0:E * I].rearrange("h (e i) -> h e i", e=E), ed_w.rearrange("e h i -> h e i"), w2_loaded)
            load(raw_d[:, E * I:], sd_w, w2_loaded)

            for b in range(1, B):
                load(x_batch(b), x_rows[b], x_loaded[b])

            sp.wait_ge(s["gabo_split"], 5)
            sp.wait_ge(s["dve_const"], 2)
            for k in range(3):
                load(gabo_parts[32 * k:32 * k + 1, :].rearrange("o (b d) -> o b d", d=D), gabo_p[:, k, :],
                     gabo_moved)

            def store_h2T(b, half):
                _, _, last = at(b, 4 * half + 3, 0)
                sp.wait_ge(s["h2T_done"], last + 1)
                sp.dma_start(h2T_all[:, bass.ds(b * (CPB * P) + half * 512, 512)],
                             h2T_w[:, 4 * half:4 * half + 4, :]).then_inc(h2T_stored[half], 16)

            with sp.Fori(0, B) as b:
                for half in range(2):
                    store_h2T(b, half)

            with sp.Fori(0, B) as b:
                for t in range(2):
                    sp.wait_ge(s["fin_done"], 2 * b + t + 1)
                    sp.dma_start(out_rows[bass.ds(b, 1), t][0],
                                 x_all[:, bass.ds(b * (CPB * P) + t * 512, 512)]
                                 .rearrange("p (c d) -> p c d", d=D)).then_inc(out_stored, 16)
            for half in range(2):
                sp.wait_ge(h2T_stored[half], 16 * B)
            sp.wait_ge(out_stored, 16 * TILES)

        @block.gpsimd
        def _(pool):
            n = [0]

            def made(ins, wait=True):
                ins.then_inc(s["const_ident"], 1)
                n[0] += 1
                if wait:
                    pool.wait_ge(s["const_ident"], n[0])

            made(nc.gpsimd.memset(ident[:], 0.0))
            made(nc.gpsimd.affine_select(out=ident[:], in_=ident[:], compare_op=ALU.not_equal, fill=1.0,
                                         base=0, pattern=[[-1, P]], channel_multiplier=1))
            made(nc.gpsimd.tensor_copy(ident_b[:], ident[:]))
            made(nc.gpsimd.memset(tri[:], 1.0))
            made(nc.gpsimd.affine_select(out=tri[:], in_=tri[:], compare_op=ALU.is_ge, fill=0.0,
                                         base=0, pattern=[[1, P]], channel_multiplier=-1))
            hm = head_mask[:].rearrange("p (h m) -> p h m", m=HV)
            made(nc.gpsimd.memset(head_mask[:], 1.0))
            made(nc.gpsimd.affine_select(out=hm, in_=hm, compare_op=ALU.is_ge, fill=0.0,
                                         base=0, pattern=[[-HD, HEADS], [0, HV]], channel_multiplier=1))
            made(nc.gpsimd.affine_select(out=hm, in_=hm, compare_op=ALU.is_ge, fill=0.0,
                                         base=HD - 1, pattern=[[HD, HEADS], [0, HV]], channel_multiplier=-1))
            made(nc.gpsimd.memset(spread[:], 1.0))
            made(nc.gpsimd.affine_select(out=spread[:], in_=spread[:], compare_op=ALU.is_equal, fill=0.0,
                                         base=0, pattern=[[-1, B], [0, P]], channel_multiplier=1))
            made(nc.gpsimd.memset(pick[:], -MASKED_OUT))
            made(nc.gpsimd.affine_select(out=pick[:], in_=pick[:], compare_op=ALU.is_equal, fill=0.0,
                                         base=0, pattern=[[2, UNITS - 1], [1, 2], [0, I]], channel_multiplier=-1))
            made(nc.gpsimd.iota(order[:], pattern=[[-1, E]], base=E, channel_multiplier=0,
                                allow_small_or_imprecise_dtypes=True))
            made(nc.gpsimd.memset(x_all[:, NCH * P:], 0.0))
            nc.gpsimd.memset(ones_f[:], 1.0).then_inc(s["const_all"], 1)

            def norm_factors(pair, par, lo, hi):
                if isinstance(pair, int) and pair == 0:
                    pool.wait_ge(s["dve_const"], 2)
                pool.wait_ge(s["agg_done"], stat_before(pair) + hi - lo)
                wait_count(pool, "ln_done", pair)
                nc.gpsimd.tensor_tensor(neg_mean[:, lo:hi], agg[:, par, lo:hi, 0], minus_1[:, lo:hi], ALU.mult)
                nc.gpsimd.tensor_tensor(ve[:, lo:hi], agg[:, par, lo:hi, 1], eps[:, lo:hi], ALU.add)\
                    .then_inc(s["ve_done"], 1)
                pool.wait_ge(s["ve_done"], pair + 1)
                wait_count(pool, "xn_done", 2 * pair - 2, NCH)
                wait_count(pool, "xn2_done", 2 * pair - 10)
                nc.gpsimd.tensor_tensor(rstd[:, par, lo:hi], ve[:, lo:hi], half_m[:, lo:hi], ALU.pow)\
                    .then_inc(s["rstd_done"], 1)
                pool.wait_ge(s["rstd_done"], pair + 1)
                nc.gpsimd.tensor_tensor(nmr[:, par, lo:hi], neg_mean[:, lo:hi], rstd[:, par, lo:hi], ALU.mult)\
                    .then_inc(s["ln_done"], 1)

            def step(b, c):
                _, c2, n2 = at(b, c, 2)
                if not isinstance(n2, int) or 0 <= n2 < NCH:
                    pool.wait_ge(s["elu_done"], n2 + 1)
                    pool.wait_ge(s["v_done"], n2 + 1)
                    if not isinstance(n2, int) or n2 >= 2:
                        pool.wait_ge(s["C_done"], 3 * n2 - 3)
                    k_b = qk[:, c2 % 4, P:2 * P].rearrange("p (h d o) -> p h d o", h=HEADS, o=1)
                    v_b = v_aug[:, c2 % 4].rearrange("p h (o m) -> p h o m", o=1)
                    shape = [P, HEADS, HD, HV]
                    nc.gpsimd.tensor_tensor(kv[:, c2 % 2, :].rearrange("p (h d m) -> p h d m", h=HEADS, d=HD),
                                            k_b.broadcast_to(shape), v_b.broadcast_to(shape),
                                            ALU.mult).then_inc(s["kv_done"], 1)
                if c % 2 == 1 and (not isinstance(b, int) or b * CPB + c - 1 <= NCH + 4):
                    lo, hi = pair_cols(b, c - 1)
                    norm_factors(b * 4 + c // 2 + 1, (c // 2 + 1) % 2, lo, hi)
                b3, c3, n = at(b, c, 3)
                if valid(n) and c3 < CPB - 1:
                    pool.wait_ge(s["s_read"], 7 * b3 + c3 + 1)
                    wait_count(pool, "inter_done", 7 * b3 + c3 - 1)
                    nc.gpsimd.tensor_tensor(s_bd[:, c3 % 2, :], s_full[:], head_mask[:], ALU.mult)\
                        .then_inc(s["sbd_done"], 1)

            norm_factors(0, 0, 0, 2)
            for c in range(CPB):
                step(0, c)
            with pool.Fori(1, B) as b:
                for c in range(CPB):
                    step(b, c)
            for c in range(CPB):
                step(B, c)

        @block.tensor
        def _(pe):
            mm = nc.tensor.matmul
            pe.wait_ge(w_loaded, 160)
            pe.wait_ge(s["const_ident"], 2)
            nc.tensor.transpose(ps_t[:, 0:B], cond_sb[:], ident[0:B, 0:B]).then_inc(s["setup_pe"], 1)
            pe.wait_ge(s["setup_dve"], 3)
            for k in (0, 1, 3, 4):
                last = mm(ps_a[:, k * B:(k + 1) * B], wmod_sb[:, ts(k, D)], condT[:, 2, :], start=True, stop=True)
            last.then_inc(s["setup_pe"], 1)
            for i, k in enumerate((2, 5)):
                last = mm(ps_q[0:B, ts(i, D)], condT[:, 2, :], wmod_sb[:, ts(k, D)], start=True, stop=True)
            last.then_inc(s["setup_pe"], 1)
            pe.wait_ge(s["setup_act"], 3)
            pe.wait_ge(s["const_all"], 1)
            pe.wait_ge(s["dve_const"], 1)
            pe.wait_ge(s["setup_dve"], 10)

            def spread_g(k, banks, ready):
                for half in range(2):
                    for b in range(4):
                        last = mm(banks[half][:, ts(b, D)], spread[:, 4 * half + b, :], g8[:, ts(k, D)],
                                  start=True, stop=True)
                last.then_inc(ready, 1)

            def step(b, c):
                _, c1, r = at(b, c, 1)
                if valid(r):
                    pe.wait_ge(s["hT_done"], r + 1)
                    wait_count(pe, "elu_done", r)
                    wait_count(pe, "v_done", r)
                    mm(ps_a[:, 0:3 * P], ones_b[:], bias_parts[:], start=True, stop=False)
                    mm(ps_a[:, 0:3 * P], hT[:, c1 % 2, :], w_qkv[:], start=False, stop=True)\
                        .then_inc(s["qkv_done"], 1)
                _, c3, q = at(b, c, 3)
                _, c5, v = at(b, c, 5)
                if valid(q):
                    pe.wait_ge(s["elu_done"], q + 1)
                if valid(q) or valid(v):
                    wait_count(pe, "qT_done", q, NCH)
                    wait_count(pe, "valT_done", v)
                if valid(q):
                    nc.tensor.transpose(ps_q[:, 0:P], qk[:, c3 % 4, 0:P], ident[:]).then_inc(s["qT_ps"], 1)
                if valid(v):
                    pe.wait_ge(s["norm_done"], v + 1)
                    nc.tensor.transpose(ps_q[:, P:2 * P], val[:, c5 % 2, :], ident[:]).then_inc(s["valT_ps"], 1)
                _, c0, a = at(b, c, 0)
                _, c8, u = at(b, c, 8)
                if valid(u):
                    pe.wait_ge(s["xn2_done"], u + 1)
                    wait_count(pe, "hT_done", a, NCH)
                    wait_count(pe, "logits_done", u)
                    nc.tensor.transpose(ps_t[:, 128:256], xn2[:, c8 % 2, :], ident[:]).then_inc(s["xn2T_ps"], 1)
                b3, c3, n = at(b, c, 3)
                if valid(n):
                    pe.wait_ge(s["kv_done"], n + 1)
                    for k, (h0, h1) in enumerate(THIRDS):
                        wait_count(pe, "qm_done", 3 * n - 2 + k)
                        w = HD * HV
                        mm(ps_c[k][:, 0:(h1 - h0) * w], tri[:], kv[:, c3 % 2, h0 * w:h1 * w],
                           start=True, stop=True).then_inc(s["C_done"], 1)
                    if c3 < CPB - 1:
                        wait_count(pe, "s_read", 7 * b3 + c3)
                        mm(ps_s[:, 0:FV], qk[:, c3 % 4, P:2 * P], v_aug[:, c3 % 4].rearrange("p h m -> p (h m)"),
                           start=(c3 == 0), stop=True, skip_group_check=True).then_inc(s["ktv_done"], 1)
                if valid(a):
                    pe.wait_ge(s["xn_done"], a + 1)
                    wait_count(pe, "hT_done", a)
                wait_count(pe, "logits_done", u)
                if valid(u):
                    pe.wait_ge(s["h2T_done"], u + 1)
                if valid(a):
                    nc.tensor.transpose(ps_t[:, 0:P], xn[:, c0 % 2, :], ident[:]).then_inc(s["xnT_done"], 1)
                if valid(u):
                    mm(ps_t[:, 256:256 + E], h2T_w[:, c8, :], rwT[:], start=True, stop=True)\
                        .then_inc(s["logits_ps"], 1)
                b5, c5, m = at(b, c, 5)
                if valid(m) or valid(n):
                    wait_count(pe, "x1_done", m)
                    wait_count(pe, "add_done", 7 * b3 + max(c3 - 1, 0), 7 * B)
                if valid(m):
                    pe.wait_ge(s["valT_done"], m + 1)
                    pe.wait_ge(s["woga_done"], b5 + 1)
                    mm(ps_i[:, 256:384], ones_b[:], gabo_parts[:, ts(b5, D)], start=True, stop=False)
                    mm(ps_i[:, 256:384], valT[:, c5 % 2, :], w_o_ga[:], start=False, stop=True)\
                        .then_inc(s["y_done"], 1)
                if valid(n) and c3 > 0:
                    pe.wait_ge(s["qT_done"], n + 1)
                    pe.wait_ge(s["sbd_done"], 7 * b3 + c3)
                    mm(ps_i[:, 0:FV], qT[:, c3 % 2, :], s_bd[:, (c3 - 1) % 2, :],
                       start=True, stop=True).then_inc(s["inter_done"], 1)

            step(0, 0)
            pe.wait_ge(s["setup_dve"], 14)
            spread_g(0, (ps_i, ps_s), s["setup_pe"])
            pe.wait_ge(w2_loaded, 128)
            nc.tensor.transpose(ps_c[0][:, 0:E], raw_r[:], ident[0:E, 0:E]).then_inc(s["setup_pe"], 1)
            step(0, 1)
            step(0, 2)
            pe.wait_ge(s["setup_act"], 4)
            for c in range(3, CPB):
                if c == 5:
                    pe.wait_ge(gabo_moved, 48)
                step(0, c)
            with pe.Fori(1, B) as b:
                for c in range(CPB):
                    step(b, c)
            for c in range(CPB):
                step(B, c)

            pe.wait_ge(s["qm_done"], 3 * NCH)
            pe.wait_ge(s["x1_done"], NCH)
            pe.wait_ge(s["add_done"], 7 * B)
            pe.wait_ge(s["s_read"], 7 * B)
            pe.wait_ge(w2_loaded, 128)
            for bank_, shared, raw in ((ps_c[0], 0, raw_g), (ps_c[1], 1, raw_u), (ps_c[2], 2, raw_d)):
                for u in range(UNITS):
                    src = raw[:, u, :] if raw is not raw_d else raw_d[:, ts(u, P)]
                    dst = bank_[:, ts(u, P)] if u < 4 else ps_i[:, ts(shared, P)]
                    last = nc.tensor.transpose(dst, src, ident[:])
            last.then_inc(s["gate_pe"], 1)
            spread_g(1, (ps_s, ps_q), s["gb_ps"])
            pe.wait_ge(s["gate_dve"], 21)
            mm(ps_a[:, 0:2 * E], ones_f[:], tot[:], start=True, stop=True).then_inc(s["gate_pe"], 1)
            def choice(b, first):
                pe.wait_ge(s["selw_done"], b + 1)
                if not first:
                    pe.wait_ge(s["selT_done"], b)
                sel_ps = ps_q[:].bitcast(BF16)
                for j in range(CPB):
                    last = nc.tensor.transpose(sel_ps[0:E, ts(j, P)], sel_w[:, ts(j, E)], ident_b[:])
                last.then_inc(s["selT_ps"], 1)

            pe.wait_ge(s["gb_done"], 1)
            choice(0, True)
            with pe.Fori(1, B) as b:
                choice(b, False)
            pe.wait_ge(s["selT_done"], B)
            pe.wait_ge(s["gate_dve"], 25)
            pe.wait_ge(s["gate_act"], 5)

            def gate_up(b, i):
                b, i = (b + 1, i - 10) if i >= 10 else (b, i)
                t, u = divmod(i, UNITS)
                m = b * 10 + i
                h2 = h2T_all[:, bass.ds(b * (CPB * P) + t * 512, 512)]
                wait_count(pe, "silu_done", m - 1)
                mm(ps_g[i % 2][:], gwT[:, u, :], h2, start=True, stop=(u == UNITS - 1))\
                    .then_inc(s["g_done"], 1)
                if u < UNITS - 1:
                    mm(ps_g[i % 2][:], pick[:, u].rearrange("e a i -> e (a i)"),
                       selT[:, bass.ds(b * (CPB * P) + t * 512, 512)], start=False, stop=True)\
                        .then_inc(s["g_done"], 1)
                wait_count(pe, "hid_done", m - 1)
                mm(ps_u[i % 2][:], uwT[:, u, :], h2, start=True, stop=True).then_inc(s["u_done"], 1)

            def down(b, i):
                t, u = divmod(i, UNITS)
                m = b * 10 + i
                pe.wait_ge(s["hid_done"], m + 1)
                if u == 0:
                    wait_count(pe, "ffn_done", 2 * b + t - 1)
                for j in range(4):
                    last = mm(ps_o[t][:, ts(j, P)], hid[:, i % 2, ts(j, P)], dwT[:, u, :],
                              start=(u == 0 and j == 0), stop=(u == UNITS - 1), skip_group_check=True)
                last.then_inc(s["down_done"], 1)

            def expert_row(b, last_row):
                for i in range(10):
                    if not (last_row and i == 9):
                        gate_up(b, i + 1)
                    down(b, i)

            for h in range(2):
                pe.wait_ge(h2T_stored[h], 16 * B)
            gate_up(0, 0)
            expert_row(0, False)
            with pe.Fori(1, B - 1) as b:
                expert_row(b, False)
            expert_row(B - 1, True)

        @block.scalar
        def _(act):
            A = nc.scalar.activation
            act.wait_ge(s["setup_pe"], 1)
            act.wait_ge(s["dve_const"], 1)
            A(condT[:, 0, :], ps_t[:, 0:B], ACT.Exp, scale=-1.0).then_inc(s["setup_act"], 1)
            act.wait_ge(s["setup_pe"], 2)
            A(modT[:, 0:2, :].rearrange("p k b -> p (k b)"), ps_a[:, 0:2 * B], ACT.Copy)
            A(modT[:, 3:5, :].rearrange("p k b -> p (k b)"), ps_a[:, 3 * B:5 * B], ACT.Copy)\
                .then_inc(s["setup_act"], 1)
            act.wait_ge(s["setup_pe"], 3)
            A(g_raw[:], ps_q[0:B, 0:2 * D], ACT.Copy).then_inc(s["setup_act"], 1)
            act.wait_ge(s["setup_dve"], 4)

            def xn1(b, c):
                a_b, a_c, a = b, c, b * CPB + c
                if c == CPB:
                    a_b, a_c, a = b + 1, 0, (b + 1) * CPB
                if isinstance(a, int) and a >= NCH:
                    return
                pair = b * 4 + c // 2
                act.wait_ge(s["ln_done"], pair + 1)
                wait_count(act, "xnT_done", a - 1)
                par, col = (c // 2) % 2, c % 2
                A(xn[:, a_c % 2, :], x_all[:, ts(a, P)], ACT.Identity, bias=nmr[:, par, col:col + 1],
                  scale=rstd[:, par, col:col + 1]).then_inc(s["xn_done"], 1)

            def step(b, c):
                _, c1, r = at(b, c, 1)
                if valid(r):
                    act.wait_ge(s["qkv_done"], r + 1)
                    bk_, ck_, _ = at(b, c, 5)
                    wait_count(act, "ktv_done", 7 * bk_ + min(ck_ + 1, 7))
                    wait_count(act, "kv_done", r - 3)
                    A(v_aug[:, c1 % 4, :, 0:HD], ps_a[:, 2 * P:3 * P].rearrange("p (h m) -> p h m", m=HD),
                      ACT.Copy).then_inc(s["v_done"], 1)
                    wait_count(act, "elu_done", r - 1)
                    A(e_qk[:, c1 % 2, :], ps_a[:, 0:2 * P], ACT.Exp, bias=neg1[:]).then_inc(s["exp_done"], 1)
                _, c3, q = at(b, c, 3)
                b5, c5, v = at(b, c, 5)
                if valid(v):
                    act.wait_ge(s["valT_ps"], v + 1)
                if valid(q):
                    act.wait_ge(s["qT_ps"], q + 1)
                    wait_count(act, "inter_done", 7 * b5 + c5)
                    A(qT[:, c3 % 2, :], ps_q[:, 0:P], ACT.Copy).then_inc(s["qT_done"], 1)
                if valid(v):
                    wait_count(act, "y_done", v - 1)
                    A(valT[:, c5 % 2, :], ps_q[:, P:2 * P], ACT.Copy).then_inc(s["valT_done"], 1)
                b8, c8, u = at(b, c, 8)
                if valid(u):
                    act.wait_ge(s["xn2T_ps"], u + 1)
                    if c8 == 0:
                        A(mod2[:], modT[:, 3:5, bass.ds(b8, 1)].rearrange("p k o -> p (k o)"), ACT.Copy)\
                            .then_inc(s["mod2_done"], 1)
                        act.wait_ge(s["mod2_done"], b8 + 1)
                    if not isinstance(b8, int) or b8 > 0:
                        act.wait_ge(h2T_stored[c8 // 4], b8 * 16)
                    A(h2T_w[:, c8, :], ps_t[:, 128:256], ACT.Identity, bias=mod2[:, 0:1],
                      scale=mod2[:, 1:2]).then_inc(s["h2T_done"], 1)
                b3, c3, n = at(b, c, 3)
                if valid(n) and c3 < CPB - 1:
                    act.wait_ge(s["ktv_done"], 7 * b3 + c3 + 1)
                    wait_count(act, "sbd_done", 7 * b3 + c3)
                    A(s_full[:], ps_s[:, 0:FV], ACT.Copy).then_inc(s["s_read"], 1)
                _, c0, a = at(b, c, 0)
                if valid(a) and c == 0:
                    A(mod1[:], modT[:, 0:2, bass.ds(b, 1)].rearrange("p k o -> p (k o)"), ACT.Copy)\
                        .then_inc(s["mod1_done"], 1)
                    act.wait_ge(s["mod1_done"], b + 1)
                if valid(u):
                    act.wait_ge(s["logits_ps"], u + 1)
                if valid(a):
                    act.wait_ge(s["xnT_done"], a + 1)
                    wait_count(act, "qkv_done", a - 1)
                    A(hT[:, c0 % 2, :], ps_t[:, 0:P], ACT.Identity, bias=mod1[:, 0:1],
                      scale=mod1[:, 1:2]).then_inc(s["hT_done"], 1)
                if valid(u):
                    A(logits[:, ts(u, E)], ps_t[:, 256:256 + E], ACT.Copy).then_inc(s["logits_done"], 1)
                xn1(b, c + 1)
                _, c7, w = at(b, c, 7)
                if valid(w):
                    j = c7 % 2
                    pair = b * 4 + (c - 1) // 2 + 1 if c else b * 4
                    act.wait_ge(s["ln_done"], pair + 1)
                    wait_count(act, "xn2T_ps", w - 1)
                    par = pair_par(c)
                    A(xn2[:, j, :], x_all[:, ts(w, P)], ACT.Identity, bias=nmr[:, par, 2 + j:3 + j],
                      scale=rstd[:, par, 2 + j:3 + j]).then_inc(s["xn2_done"], 1)

            xn1(0, 0)
            step(0, 0)
            act.wait_ge(s["setup_pe"], 5)
            A(ga_bc[:, 0:512], ps_i[:], ACT.Copy)
            A(ga_bc[:, 512:1024], ps_s[:], ACT.Copy)
            A(rwT[:], ps_c[0][:, 0:E], ACT.Copy).then_inc(s["setup_act"], 1)
            for c in range(1, CPB):
                step(0, c)
            with act.Fori(1, B) as b:
                for c in range(CPB):
                    step(b, c)
            for c in range(CPB):
                step(B, c)

            act.wait_ge(s["gate_pe"], 1)
            A(gwT[:, 0:4, :].rearrange("p u d -> p (u d)"), ps_c[0][:], ACT.Copy).then_inc(s["gate_act"], 1)
            A(uwT[:, 0:4, :].rearrange("p u d -> p (u d)"), ps_c[1][:], ACT.Copy).then_inc(s["gate_act"], 1)
            A(dwT[:, 4, :], ps_i[:, 256:384], ACT.Copy)
            A(gwT[:, 4, :], ps_i[:, 0:128], ACT.Copy)
            A(uwT[:, 4, :], ps_i[:, 128:256], ACT.Copy).then_inc(s["gate_act"], 1)
            act.wait_ge(s["gate_dve"], 1)
            A(gl[1][:], gl[0][:], ACT.Exp, scale=-1.0).then_inc(s["gate_act"], 1)

            A(dwT[:, 0:4, :].rearrange("p u d -> p (u d)"), ps_c[2][:], ACT.Copy).then_inc(s["gate_act"], 1)

            act.wait_ge(s["gb_ps"], 1)
            A(gb_bc[:, 0:512], ps_s[:], ACT.Copy)
            A(gb_bc[:, 512:1024], ps_q[:], ACT.Copy).then_inc(s["gb_done"], 1)

            def choice(b):
                act.wait_ge(s["selT_ps"], b + 1)
                A(selT[:, ts(b, CPB * P)], ps_q[0:E, :].bitcast(BF16), ACT.Copy).then_inc(s["selT_done"], 1)

            with act.Fori(0, B) as b:
                choice(b)

            def expert_row(b):
                for i in range(10):
                    m = b * 10 + i
                    masks = i + 1 - (i + 1) // UNITS
                    act.wait_ge(s["g_done"], b * 18 + i + 1 + masks)
                    wait_count(act, "hid_done", m - 1)
                    A(silu_g[:, i % 2, :], ps_g[i % 2][:], ACT.Silu).then_inc(s["silu_done"], 1)

            expert_row(0)
            with act.Fori(1, B) as b:
                expert_row(b)

        @block.vector
        def _(dve):
            V = nc.vector
            V.memset(neg1[:], -1.0)
            V.memset(ones_b[:], 1.0)
            V.memset(v_aug[:], 1.0)
            V.memset(bias_parts[:], 0.0)
            V.memset(gabo_parts[:], 0.0).then_inc(s["dve_const"], 1)
            V.memset(minus_1[:], -1.0)
            V.memset(eps[:], LN_EPS)
            V.memset(half_m[:], -0.5).then_inc(s["dve_const"], 1)
            def statistics(lo, hi, chunks):
                for col in range(lo, hi):
                    V.bn_stats(st[:, col, :], x_all[:, ts(chunks[col], P)]).then_inc(s["stat_done"], 1)

            def mean_var(par, lo, hi):
                for col in range(lo, hi):
                    V.bn_aggr(agg[:, par, col, :], st[:, col, :]).then_inc(s["agg_done"], 1)

            def step(b, c):
                is_reg = not isinstance(b, int)
                no = b * CPB + c
                _, c1, r = at(b, c, 1)
                b3, c3, n = at(b, c, 3)
                b4, c4, v = at(b, c, 4)
                b5, c5, m = at(b, c, 5)

                def stats_wait():
                    if c % 2 == 1 and (is_reg or no - 1 <= NCH + 4):
                        pair = b * 4 + c // 2 + 1
                        dve.wait_ge(s["stat_done"], stat_before(pair + 1))
                        wait_count(dve, "ln_done", pair - 1)

                if not valid(r):
                    stats_wait()
                if valid(r):
                    dve.wait_ge(s["exp_done"], r + 1)
                    wait_count(dve, "kv_done", r - 3)
                    wait_count(dve, "ktv_done", 7 * b5 + min(c5 + 1, 7))
                    wait_count(dve, "qT_ps", r - 3)
                    stats_wait()
                    V.scalar_tensor_tensor(out=qk[:, c1 % 4, :], in0=e_qk[:, c1 % 2, :], scalar=1.0,
                                           in1=ps_a[:, 0:2 * P], op0=ALU.min, op1=ALU.max).then_inc(s["elu_done"], 1)

                if c % 2 == 1 and (is_reg or no - 1 <= NCH + 4):
                    lo, hi = pair_cols(b, c - 1)
                    mean_var((c // 2 + 1) % 2, lo, hi)

                def times_q(k):
                    if valid(n):
                        h0, h1 = THIRDS[k]
                        rows = (h1 - h0) * HD
                        dve.wait_ge(s["C_done"], 3 * n + k + 1)
                        V.tensor_tensor(prod[:, h0 * HD * HV:h1 * HD * HV].rearrange("p (r m) -> p r m", m=HV),
                                        ps_c[k][:, 0:rows * HV].rearrange("p (r m) -> p r m", m=HV),
                                        qk[:, c3 % 4, h0 * HD:h1 * HD].rearrange("p (r o) -> p r o", o=1)
                                        .broadcast_to([P, rows, HV]), ALU.mult).then_inc(s["qm_done"], 1)

                num = (nd if c4 > 0 else red)[:].rearrange("p (h m) -> p h m", m=HV)
                wait_count(dve, "red_done", min(n, NCH) if isinstance(n, int) else n)
                times_q(0)
                if valid(v):
                    wait_count(dve, "add_done", 7 * b4 + c4)
                    wait_count(dve, "rec_done", v)
                    V.tensor_scalar(den[:], num[:, :, HD], 1e-6, None, ALU.add).then_inc(s["den_done"], 1)
                times_q(1)
                if valid(v):
                    dve.wait_ge(s["den_done"], v + 1)
                    wait_count(dve, "norm_done", v)
                    V.reciprocal(rec[:], den[:]).then_inc(s["rec_done"], 1)
                times_q(2)
                if valid(v):
                    dve.wait_ge(s["rec_done"], v + 1)
                    wait_count(dve, "valT_ps", v - 1)
                    V.tensor_tensor(val[:, c4 % 2, :].rearrange("p (h m) -> p h m", m=HD), num[:, :, 0:HD],
                                    rec[:].rearrange("p (h o) -> p h o", o=1).broadcast_to([P, HEADS, HD]),
                                    ALU.mult).then_inc(s["norm_done"], 1)

                def attention_out():
                    if not valid(m):
                        return
                    dve.wait_ge(s["y_done"], m + 1)
                    if valid(n) and c3 > 0:
                        dve.wait_ge(s["inter_done"], 7 * b3 + c3)
                    V.tensor_tensor(x_all[:, ts(m, P)], ps_i[:, 256:384], x_all[:, ts(m, P)], ALU.add)\
                        .then_inc(s["x1_done"], 1)
                    if c5 == CPB - 1 and (is_reg or b < B):
                        V.tensor_tensor(w_o_ga[:], w_o[:], ga_bc[:, ts(b, D)], ALU.mult).then_inc(s["woga_done"], 1)

                def sum_over_d():
                    if not valid(n):
                        return
                    dve.wait_ge(s["qm_done"], 3 * n + 3)
                    if c4 == 0:
                        wait_count(dve, "norm_done", n)
                    V.tensor_reduce(red[:].rearrange("p (h m) -> p h m", m=HV),
                                    prod[:].rearrange("p (h d m) -> p h m d", d=HD, m=HV), AX_X, ALU.add)\
                        .then_inc(s["red_done"], 1)

                pairs = c % 2 == 0 and (is_reg or no <= NCH + 4)
                if c % 2 == 0:
                    attention_out()
                    sum_over_d()
                else:
                    sum_over_d()
                    attention_out()
                if pairs:
                    lo, hi = pair_cols(b, c)
                    pair = b * 4 + c // 2 + 1
                    dve.wait_ge(s["agg_done"], stat_before(pair))
                    if hi == 4:
                        dve.wait_ge(s["x1_done"], no - 4)
                    statistics(lo, hi, [no + 2, no + 3, no - 6, no - 5])
                if valid(n) and c3 > 0:
                    dve.wait_ge(s["red_done"], n + 1)
                    dve.wait_ge(s["inter_done"], 7 * b3 + c3)
                    V.tensor_tensor(nd[:], ps_i[:, 0:FV], red[:], ALU.add).then_inc(s["add_done"], 1)

            dve.wait_ge(x_loaded[0], 16)
            statistics(0, 2, [0, 1])
            dve.wait_ge(s["stat_done"], 2)
            mean_var(0, 0, 2)
            dve.wait_ge(s["setup_act"], 1)
            V.tensor_scalar(condT[:, 0, :], condT[:, 0, :], 1.0, None, ALU.add).then_inc(s["setup_dve"], 1)
            dve.wait_ge(s["setup_dve"], 1)
            V.reciprocal(condT[:, 1, :], condT[:, 0, :]).then_inc(s["setup_dve"], 1)
            dve.wait_ge(s["setup_dve"], 2)
            V.tensor_tensor(condT[:, 2, :], ps_t[:, 0:B], condT[:, 1, :], ALU.mult).then_inc(s["setup_dve"], 1)
            dve.wait_ge(s["setup_act"], 2)
            V.tensor_scalar(modT[:, 1, :], modT[:, 1, :], 1.0, None, ALU.add)
            V.tensor_scalar(modT[:, 4, :], modT[:, 4, :], 1.0, None, ALU.add)\
                .then_inc(s["setup_dve"], 1)
            V.tensor_scalar(bias_row[0:1, 0:2 * P], bias_row[0:1, 0:2 * P], 1.0, None, ALU.add)\
                .then_inc(s["setup_dve"], 1)
            dve.wait_ge(s["setup_dve"], 5)
            split_row(dve, lambda k: bias_parts[32 * k:32 * k + 1, 0:3 * P], bias_row, 1, 3 * P, s["setup_dve"], 5)
            dve.wait_ge(s["setup_act"], 3)
            V.tensor_scalar(g_sgn[:], g_raw[:], 0.0, 2.0, ALU.is_ge, ALU.mult).then_inc(s["setup_dve"], 1)
            dve.wait_ge(s["setup_dve"], 11)
            V.tensor_scalar(g_sgn[:], g_sgn[:], -1.0, None, ALU.add).then_inc(s["setup_dve"], 1)
            dve.wait_ge(s["setup_dve"], 12)
            V.tensor_tensor(g_raw[:], g_raw[:], g_sgn[:], ALU.mult).then_inc(s["setup_dve"], 1)
            dve.wait_ge(s["setup_dve"], 13)
            V.scalar_tensor_tensor(out=g8[:], in0=g_raw[:], scalar=0.25, in1=g_sgn[:], op0=ALU.max, op1=ALU.mult)\
                .then_inc(s["setup_dve"], 1)
            dve.wait_ge(s["setup_dve"], 14)
            V.tensor_tensor(gabo[:], g8[:, 0:D], bo_8[:], ALU.mult).then_inc(s["setup_dve"], 1)
            dve.wait_ge(s["setup_dve"], 15)
            split_row(dve, lambda k: gabo_p[:, k, :], gabo, B, D, s["gabo_split"], 0)

            dve.wait_ge(s["const_all"], 1)
            for c in range(CPB):
                if c == 3:
                    dve.wait_ge(s["setup_act"], 4)
                    V.tensor_tensor(w_o_ga[:], w_o[:], ga_bc[:, 0:D], ALU.mult).then_inc(s["woga_done"], 1)
                if c == 6:
                    dve.wait_ge(x_loaded[1], 16)
                step(0, c)
            for b in range(2, B):
                dve.wait_ge(x_loaded[b], 16)
            with dve.Fori(1, B) as b:
                for c in range(CPB):
                    step(b, c)
            for c in range(CPB):
                step(B, c)

            n = [0]

            def link(ins):
                ins.then_inc(s["gate_dve"], 1)
                n[0] += 1
                dve.wait_ge(s["gate_dve"], n[0])

            def by_chunk(t):
                return t.rearrange("p (n e) -> p n e", e=E)

            def over_e(t):
                return t.rearrange("p (n o) -> p n o", o=1).broadcast_to([P, NCH, E])

            row = [P, NCH, E]
            order_b = order[:].rearrange("p (o e) -> p o e", o=1).broadcast_to(row)
            dve.wait_ge(s["logits_done"], NCH)
            link(V.tensor_tensor(by_chunk(gl[0][:]), by_chunk(logits[:]),
                                 lb_bc[:].rearrange("p (o e) -> p o e", o=1).broadcast_to(row), ALU.add))
            dve.wait_ge(s["gate_act"], 4)
            link(V.tensor_scalar(gl[1][:], gl[1][:], 1.0, None, ALU.add))
            link(V.reciprocal(gl[0][:], gl[1][:]))
            for k in range(2):
                best, mk, one = gm[:, k, :], gm[:, 2 + k, :], gl[2 + k]
                link(V.tensor_reduce(best, by_chunk(gl[0][:]), AX_X, ALU.max))
                link(V.tensor_tensor(by_chunk(gl[4][:]), by_chunk(gl[0][:]), over_e(best), ALU.is_equal))
                link(V.tensor_tensor(by_chunk(gl[4][:]), by_chunk(gl[4][:]), order_b, ALU.mult))
                link(V.tensor_reduce(mk, by_chunk(gl[4][:]), AX_X, ALU.max))
                link(V.tensor_tensor(by_chunk(one[:]), by_chunk(gl[4][:]), over_e(mk), ALU.is_equal))
                if k == 0:
                    link(V.scalar_tensor_tensor(out=gl[0][:], in0=one[:], scalar=-4.0, in1=gl[0][:],
                                                op0=ALU.mult, op1=ALU.add))
            link(V.scalar_tensor_tensor(out=gm[:, 4, :], in0=gm[:, 0, :], scalar=1e-8, in1=gm[:, 1, :],
                                        op0=ALU.add, op1=ALU.add))
            link(V.reciprocal(gm[:, 5, :], gm[:, 4, :]))
            link(V.tensor_tensor(gm[:, 0:2, :], gm[:, 0:2, :],
                                 gm[:, 5:6, :].broadcast_to([P, 2, NCH]), ALU.mult))
            link(V.tensor_tensor(by_chunk(gl[4][:]), by_chunk(gl[2][:]), over_e(gm[:, 0, :]), ALU.mult))
            link(V.tensor_tensor(by_chunk(gl[5][:]), by_chunk(gl[3][:]), over_e(gm[:, 1, :]), ALU.mult))
            V.tensor_tensor(gl[2][:], gl[2][:], gl[3][:], ALU.add)
            link(V.tensor_tensor(gl[4][:], gl[4][:], gl[5][:], ALU.add))
            V.tensor_scalar(sel_m1[:], gl[2][:], -1.0, None, ALU.add)
            V.tensor_reduce(tot[:, 0:E], gl[4][:].rearrange("p (n e) -> p e n", e=E), AX_X, ALU.add)
            link(V.tensor_reduce(tot[:, E:2 * E], gl[2][:].rearrange("p (n e) -> p e n", e=E), AX_X, ALU.add))
            def choice(b):
                wait_count(dve, "selT_ps", b)
                V.tensor_copy(sel_w[:], sel_m1[:, ts(b, CPB * E)]).then_inc(s["selw_done"], 1)

            choice(0)
            dve.wait_ge(s["gate_pe"], 2)
            link(V.tensor_scalar(wmean[:, 0, :], ps_a[:, E:2 * E], 1.0, None, ALU.max))
            link(V.reciprocal(wmean[:, 1, :], wmean[:, 0, :]))
            link(V.tensor_tensor(wmean[:, 2, :], ps_a[:, 0:E], wmean[:, 1, :], ALU.mult))
            dve.wait_ge(s["gate_act"], 5)
            for u in range(UNITS - 1):
                for a in range(2):
                    rows = slice(a * I, (a + 1) * I)
                    last = V.tensor_scalar(dwT[rows, u, :], dwT[rows, u, :], wmean[rows, 2, 2 * u + a:2 * u + a + 1],
                                           None, ALU.mult)
            link(last)
            with dve.Fori(1, B) as b:
                choice(b)

            dve.wait_ge(s["gb_done"], 1)

            def finish(tile, b, t):
                dve.wait_ge(s["down_done"], UNITS * (tile + 1))
                wait_count(dve, "fin_done", tile)
                V.tensor_tensor(ffn[:].rearrange("p (j d) -> p j d", d=D),
                                ps_o[t][:].rearrange("p (j d) -> p j d", d=D),
                                gb_bc[:, ts(b, D)].rearrange("p (o d) -> p o d", o=1).broadcast_to([P, 4, D]),
                                ALU.mult).then_inc(s["ffn_done"], 1)
                dve.wait_ge(s["ffn_done"], tile + 1)
                xs = x_all[:, bass.ds(b * (CPB * P) + t * 512, 512)]
                V.tensor_tensor(xs, xs, ffn[:], ALU.add).then_inc(s["fin_done"], 1)

            def expert_row(b):
                for i in range(10):
                    m = b * 10 + i
                    dve.wait_ge(s["silu_done"], m + 1)
                    dve.wait_ge(s["u_done"], m + 1)
                    wait_count(dve, "down_done", m - 1)
                    V.tensor_tensor(hid[:, i % 2, :], silu_g[:, i % 2, :], ps_u[i % 2][:], ALU.mult)\
                        .then_inc(s["hid_done"], 1)
                    if i == 1 and (not isinstance(b, int) or b > 0):
                        finish(2 * b - 1, b - 1, 1)
                    if i == 6:
                        finish(2 * b, b, 0)

            expert_row(0)
            with dve.Fori(1, B) as b:
                expert_row(b)
            finish(TILES - 1, B - 1, 1)


_INS = ['L0_attn_x', 'L0_attn_Wq', 'L0_attn_bq', 'L0_attn_Wk', 'L0_attn_bk', 'L0_attn_Wv', 'L0_attn_bv',
        'L0_attn_Wo', 'L0_attn_bo', 'L0_ffn_gate_w', 'L0_ffn_lb_bias', 'L0_ffn_expert_gate_w',
        'L0_ffn_expert_up_w', 'L0_ffn_expert_down_w', 'L0_ffn_shared_gate_w', 'L0_ffn_shared_up_w',
        'L0_ffn_shared_down_w', 'L0_c', 'L0_wmod']
_OUTS = [((8, 1024, 128), 'float32')]


def kernel(**inputs):
    import numpy as _np
    import concourse.bacc as _bacc
    from concourse import mybir as _mybir
    from concourse.bass_utils import run_bass_kernel_spmd as _run

    nc = _bacc.Bacc("TRN2", target_bir_lowering=False, num_devices=1)
    arrays, args = {}, []
    for name in _INS:
        a = _np.ascontiguousarray(inputs[name])
        arrays[f"in_{name}_dram"] = a
        args.append(nc.dram_tensor(f"in_{name}_dram", a.shape, _mybir.dt.from_np(a.dtype), kind="ExternalInput").ap())
    for i, (shape, dtype) in enumerate(_OUTS):
        dt = _mybir.dt.from_np(_np.dtype(dtype))
        args.append(nc.dram_tensor(f"out_{i}_dram", shape, dt, kind="ExternalOutput").ap())
    adaln_block(nc, *args)
    r = _run(nc, [arrays], core_ids=[0])
    got = tuple(r.results[0][f"out_{i}_dram"] for i in range(len(_OUTS)))
    return got[0]
```

```python
from contextlib import ExitStack

import concourse.bass as bass
from concourse import mybir

F32 = mybir.dt.float32
F32R = mybir.dt.float32r
BF16 = mybir.dt.bfloat16
ALU = mybir.AluOpType
ACT = mybir.ActivationFunctionType
AX_X = mybir.AxisListType.X
ts = bass.ts

P = 128
CPB = 8
HEADS, HD = 16, 8
HV = HD + 1
FV = HEADS * HV
KVW = HEADS * HD * HV
THIRDS = [(0, 6), (6, 11), (11, 16)]
UNITS = 5
MASKED_OUT = -1.0e30
LN_EPS = 1e-5
MOST = 3.0e38
ABOVE = 3.4e38


def at(b, c, lag):
    while lag > c:
        b, c = b - 1, c + CPB
    return b, c - lag, b * CPB + (c - lag)


def adaln_block(nc, x_in, wq, bq, wk, bk, wv, bv, wo, bo, gate_w, lb_bias, eg_w, eu_w, ed_w,
                sg_w, su_w, sd_w, cond, wmod, out):
    B, S, D = x_in.shape
    E, I, _ = eg_w.shape
    NCH = B * S // P
    assert D == P and S == CPB * P and E * I == (UNITS - 1) * P and D == HEADS * HD
    XCH = NCH + 2
    TILES = B * 2

    with ExitStack() as ctx:
        def sb(name, shape, dt=F32):
            return ctx.enter_context(nc.sbuf_tensor(name, shape, dt))

        def bank(name):
            return ctx.enter_context(nc.psum_tensor(name, [P, 512], F32))

        def sem(name):
            return ctx.enter_context(nc.semaphore(name))

        x_all = sb("x_all", [P, XCH * P])
        h2_hi = sb("h2_hi", [P, NCH * P], F32R)
        h2_lo = sb("h2_lo", [P, NCH * P], F32R)
        gw_hi = sb("gw_hi", [P, UNITS, P], F32R)
        gw_lo = sb("gw_lo", [P, UNITS, P], F32R)
        uw_hi = sb("uw_hi", [P, UNITS, P], F32R)
        uw_lo = sb("uw_lo", [P, UNITS, P], F32R)
        dw = sb("dw", [P, UNITS, P])
        dw_hi = sb("dw_hi", [P, UNITS, P], F32R)
        dw_lo = sb("dw_lo", [P, UNITS, P], F32R)
        rwT = sb("rwT", [P, E])
        gbT = sb("gbT", [P, B])
        gb_row = sb("gb_row", [P, 1])
        lb_bc = sb("lb_bc", [P, E])
        ident = sb("ident", [P, P])
        ident_b = sb("ident_b", [P, P], BF16)
        ones_f = sb("ones_f", [P, P])
        pick = sb("pick", [E, UNITS - 1, 2, I], BF16)
        order = sb("order", [P, E])
        logits = sb("logits", [P, NCH * E])
        hi_w = sb("hi_w", [P, CPB, P], F32R)
        lo_w = sb("lo_w", [P, CPB, P], F32R)

        setup = ctx.enter_context(ExitStack())

        def ss(name, shape, dt=F32):
            return setup.enter_context(nc.sbuf_tensor(name, shape, dt))

        wmod_sb = ss("wmod_sb", [P, 6 * D])
        raw_g = ss("raw_g", [P, UNITS, D])
        raw_u = ss("raw_u", [P, UNITS, D])
        raw_d = ss("raw_d", [P, UNITS * P])
        rest = ss("rest", [B, 3 * P])
        hop = ss("hop", [B, 3 * P])
        setup.close()

        router = ctx.enter_context(ExitStack())

        def sr(name, shape, dt=F32):
            return router.enter_context(nc.sbuf_tensor(name, shape, dt))

        gl = [sr(f"gl{i}", [P, NCH * E]) for i in range(5)]
        gm = sr("gm", [P, 6, NCH])
        sel_m1 = sr("sel_m1", [P, NCH * E], BF16)
        sel_w = sr("sel_w", [P, 2, 4 * E], BF16)
        tot = sr("tot", [P, 2 * E])
        room = sr("room", [P, 6 * P])

        attention = ctx.enter_context(ExitStack())

        def sa(name, shape, dt=F32):
            return attention.enter_context(nc.sbuf_tensor(name, shape, dt))

        w_qkv = sa("w_qkv", [P, 3 * P])
        w_o = sa("w_o", [P, P])
        w_o_ga = sa("w_o_ga", [P, P])
        cond_sb = sa("cond_sb", [B, D])
        condT = sa("condT", [P, 3, B])
        spread = sa("spread", [B, B, P])
        modT = sa("modT", [P, 6, B])
        mod1 = sa("mod1", [P, 2])
        mod2 = sa("mod2", [P, 2])
        ga_bc = sa("ga_bc", [P, B * D])
        g_raw = sa("g_raw", [B, D])
        g_sgn = sa("g_sgn", [B, D])
        g8 = sa("g8", [B, D])
        gb_sgn = sa("gb_sgn", [P, B])
        raw_r = sa("raw_r", [E, D])
        tri = sa("tri", [P, P])
        head_mask = sa("head_mask", [P, FV])
        ones_b = sa("ones_b", [P, P], BF16)
        neg1 = sa("neg1", [P, 1])
        bias_row = sa("bias_row", [1, 3 * P])
        bo_8 = sa("bo_8", [B, P])
        bias_parts = sa("bias_parts", [P, 3 * P], BF16)
        gabo = sa("gabo", [B, D])
        gabo_p = sa("gabo_p", [B, 3, D], BF16)
        gabo_parts = sa("gabo_parts", [P, B * D], BF16)
        st = sa("st", [P, 4, 6])
        agg = sa("agg", [P, 2, 4, 2])
        half_m = sa("half_m", [P, 4])
        minus_1 = sa("minus_1", [P, 4])
        eps = sa("eps", [P, 4])
        ve = sa("ve", [P, 4])
        neg_mean = sa("neg_mean", [P, 4])
        rstd = sa("rstd", [P, 2, 4])
        nmr = sa("nmr", [P, 2, 4])
        xn = sa("xn", [P, 2, P])
        xn2 = sa("xn2", [P, 2, P])
        hT = sa("hT", [P, 2, P])
        h2T_w = sa("h2T_w", [P, 2, P])
        e_qk = sa("e_qk", [P, 2, 2 * P])
        qk = sa("qk", [P, 4, 2 * P])
        v_aug = sa("v_aug", [P, 4, HEADS, HV])
        kv = sa("kv", [P, 2, KVW])
        qT = sa("qT", [P, 2, P])
        s_full = sa("s_full", [P, FV])
        s_bd = sa("s_bd", [P, 2, FV])
        prod = sa("prod", [P, KVW])
        red = sa("red", [P, FV])
        nd = sa("nd", [P, FV])
        den = sa("den", [P, HEADS])
        rec = sa("rec", [P, HEADS])
        val = sa("val", [P, 2, P])
        valT = sa("valT", [P, 2, P])
        attention.close()

        selT = sb("selT", [E, 2, 512], BF16)
        wmean = sb("wmean", [P, 3, E])
        wm_col = sb("wm_col", [P, UNITS - 1])
        silu_g = sb("silu_g", [P, 2, 512])
        hid = sb("hid", [P, 2, 512])
        hid_hi = sb("hid_hi", [P, 2, 512], F32R)
        hid_lo = sb("hid_lo", [P, 2, 512], F32R)
        o_sb = sb("o_sb", [P, 2, 512])

        ps_t = bank("ps_t")
        ps_a = bank("ps_a")
        ps_q = bank("ps_q")
        ps_i = bank("ps_i")
        ps_s = bank("ps_s")
        ps_c = [bank(f"ps_c{k}") for k in range(3)]
        ps_g = [ps_t, ps_a]
        ps_u = [ps_q, ps_i]
        ps_o = [ps_s, ps_c[0]]
        ps_x = ps_c[1]
        ps_m = ps_c[2]

        x_loaded = [sem(f"x_loaded{b}") for b in range(B)]
        c_loaded = sem("c_loaded")
        w_loaded = sem("w_loaded")
        w2_loaded = sem("w2_loaded")
        out_stored = sem("out_stored")
        names = """const_ident const_all dve_const gabo_split setup_pe setup_act setup_dve
            xn_done xnT_done hT_done qkv_done v_done exp_done elu_done kv_done C_done qm_done red_done
            qT_ps qT_done ktv_done s_read sbd_done inter_done add_done den_done rec_done norm_done
            valT_ps valT_done y_done x1_done woga_done stat_done agg_done ve_done rstd_done ln_done
            mod1_done mod2_done xn2_done xn2T_ps h2T_w_done h2T_done h2w_free logits_ps logits_done
            gbT_ps gb_done logits_exp router selw_done selT_ps selT_done tot_ps wm_done dwhi_done dwlo_done
            g_done u_done silu_done hid_done hi_done lo_done down_done osb_done gbrow_done back_done fin_done""".split()
        s = {n: sem(n) for n in names}
        gabo_moved = sem("gabo_moved")
        h2_stored = [sem("h2_stored0"), sem("h2_stored1")]

        def split_row(dve, part, row, rows, n, done, base):
            for k in range(3):
                src = row if k == 0 else rest
                nc.vector.tensor_copy(part(k), src[0:rows, 0:n]).then_inc(done, 1)
                dve.wait_ge(done, base + 2 * k + 1)
                if k < 2:
                    nc.vector.tensor_copy(hop[0:rows, 0:n], part(k)).then_inc(done, 1)
                    dve.wait_ge(done, base + 2 * k + 2)
                    nc.vector.tensor_tensor(rest[0:rows, 0:n], src[0:rows, 0:n], hop[0:rows, 0:n],
                                            ALU.subtract).then_inc(s["rest_done"], 1)
                    rest_count[0] += 1
                    dve.wait_ge(s["rest_done"], rest_count[0])

        s["rest_done"] = sem("rest_done")
        rest_count = [0]

        block = ctx.enter_context(nc.Block())

        SH = UNITS - 1
        UPR = 2 * UNITS
        PARTS = (0, NCH - CPB, NCH)
        CHOICE_OPS = 14
        ROUTER_OPS = 2 * CHOICE_OPS + 9

        def unit(i):
            return (i, SH) if i < 2 else divmod(i - 2, SH)

        def pair_par(c):
            return ((c - 1) // 2 + 1) % 2 if c else 0

        def pair_cols(b, c):
            if isinstance(b, int):
                step_no = b * CPB + c
                return (0 if step_no + 2 < NCH else 2), (4 if step_no >= 6 else 2)
            return 0, 4

        def stat_before(pair):
            if isinstance(pair, int):
                return sum(2 if p < 4 or p > NCH // 2 else 4 for p in range(pair))
            return 4 * pair - 8

        def logits_apart(b, c):
            return isinstance(b, int) and b == B and c > 0

        def valid(n):
            return not isinstance(n, int) or 0 <= n < NCH

        def wait_count(eng, name, value, cap=None):
            if isinstance(value, int):
                if cap is not None:
                    value = min(value, cap)
                if value <= 0:
                    return
            eng.wait_ge(s[name], value)

        @block.sync
        def _(sp):
            def load(dst, src, done):
                sp.dma_start(dst, src).then_inc(done, 16)

            x_rows = x_in.rearrange("b (c p) d -> b p c d", p=P)
            out_rows = out.rearrange("b (t c p) d -> b t p c d", p=P, c=4)

            def x_batch(b):
                return x_all[:, ts(b, CPB * P)].rearrange("p (c d) -> p c d", d=D)

            load(cond_sb[:], cond, c_loaded)
            load(wmod_sb[:], wmod, c_loaded)
            load(x_batch(0), x_rows[0], x_loaded[0])
            for k, (w, b_) in enumerate(((wq, bq), (wk, bk), (wv, bv))):
                load(w_qkv[:, ts(k, P)], w, w_loaded)
                load(bias_row[0:1, ts(k, P)], b_.rearrange("(a n) -> a n", a=1), w_loaded)
            load(w_o[:], wo, w_loaded)
            load(bo_8[:], bo.rearrange("(a n) -> a n", a=1).to_broadcast([B, P]), w_loaded)
            load(raw_r[:], gate_w, w2_loaded)
            load(lb_bc[:], lb_bias.rearrange("(a n) -> a n", a=1).to_broadcast([P, E]), w2_loaded)
            for raw, we, ws in ((raw_g, eg_w, sg_w), (raw_u, eu_w, su_w)):
                load(raw[:, 0:UNITS - 1, :], we.rearrange("e i d -> (e i) d").rearrange("(u p) d -> p u d", p=P),
                     w2_loaded)
                load(raw[:, UNITS - 1, :], ws, w2_loaded)
            load(raw_d[:, 0:E * I].rearrange("h (e i) -> h e i", e=E), ed_w.rearrange("e h i -> h e i"), w2_loaded)
            load(raw_d[:, E * I:], sd_w, w2_loaded)

            for b in range(1, B):
                load(x_batch(b), x_rows[b], x_loaded[b])

            sp.wait_ge(s["gabo_split"], 5)
            sp.wait_ge(s["dve_const"], 2)
            for k in range(3):
                load(gabo_parts[32 * k:32 * k + 1, :].rearrange("o (b d) -> o b d", d=D), gabo_p[:, k, :],
                     gabo_moved)

            with sp.Fori(0, B) as b:
                for half in range(2):
                    sp.wait_ge(s["h2w_free"], 2 + b * CPB + 4 * half + 4)
                    for whole, part in ((h2_hi, hi_w), (h2_lo, lo_w)):
                        sp.dma_start(whole[:, bass.ds(b * (CPB * P) + half * 512, 512)].bitcast(F32),
                                     part[:, 4 * half:4 * half + 4, :].bitcast(F32)).then_inc(h2_stored[half], 16)

            with sp.Fori(0, B) as b:
                for t in range(2):
                    sp.wait_ge(s["fin_done"], 2 * b + t + 1)
                    sp.dma_start(out_rows[bass.ds(b, 1), t][0],
                                 x_all[:, bass.ds(b * (CPB * P) + t * 512, 512)]
                                 .rearrange("p (c d) -> p c d", d=D)).then_inc(out_stored, 16)
            for half in range(2):
                sp.wait_ge(h2_stored[half], 32 * B)
            sp.wait_ge(out_stored, 16 * TILES)

        @block.gpsimd
        def _(pool):
            n = [0]

            def made(ins, wait=True):
                ins.then_inc(s["const_ident"], 1)
                n[0] += 1
                if wait:
                    pool.wait_ge(s["const_ident"], n[0])

            made(nc.gpsimd.memset(ident[:], 0.0))
            made(nc.gpsimd.affine_select(out=ident[:], in_=ident[:], compare_op=ALU.not_equal, fill=1.0,
                                         base=0, pattern=[[-1, P]], channel_multiplier=1))

            def norm_factors(pair, par, lo, hi):
                if isinstance(pair, int) and pair == 0:
                    pool.wait_ge(s["dve_const"], 2)
                pool.wait_ge(s["agg_done"], stat_before(pair) + hi - lo)
                wait_count(pool, "ln_done", pair)
                nc.gpsimd.tensor_tensor(ve[:, lo:hi], agg[:, par, lo:hi, 1], eps[:, lo:hi], ALU.add)\
                    .then_inc(s["ve_done"], 1)
                pool.wait_ge(s["ve_done"], pair + 1)
                wait_count(pool, "xn_done", 2 * pair - 2, NCH)
                wait_count(pool, "xn2_done", 2 * pair - 10)
                nc.gpsimd.tensor_tensor(rstd[:, par, lo:hi], ve[:, lo:hi], half_m[:, lo:hi], ALU.pow)\
                    .then_inc(s["rstd_done"], 1)
                nc.gpsimd.tensor_tensor(neg_mean[:, lo:hi], agg[:, par, lo:hi, 0], minus_1[:, lo:hi], ALU.mult)\
                    .then_inc(s["rstd_done"], 1)
                pool.wait_ge(s["rstd_done"], 2 * pair + 2)
                nc.gpsimd.tensor_tensor(nmr[:, par, lo:hi], neg_mean[:, lo:hi], rstd[:, par, lo:hi], ALU.mult)\
                    .then_inc(s["ln_done"], 1)

            def step(b, c):
                _, c2, n2 = at(b, c, 2)
                if not isinstance(n2, int) or 0 <= n2 < NCH:
                    pool.wait_ge(s["elu_done"], n2 + 1)
                    pool.wait_ge(s["v_done"], n2 + 1)
                    if not isinstance(n2, int) or n2 >= 2:
                        pool.wait_ge(s["C_done"], 3 * n2 - 3)
                    k_b = qk[:, c2 % 4, P:2 * P].rearrange("p (h d o) -> p h d o", h=HEADS, o=1)
                    v_b = v_aug[:, c2 % 4].rearrange("p h (o m) -> p h o m", o=1)
                    shape = [P, HEADS, HD, HV]
                    nc.gpsimd.tensor_tensor(kv[:, c2 % 2, :].rearrange("p (h d m) -> p h d m", h=HEADS, d=HD),
                                            k_b.broadcast_to(shape), v_b.broadcast_to(shape),
                                            ALU.mult).then_inc(s["kv_done"], 1)
                if c % 2 == 1 and (not isinstance(b, int) or b * CPB + c - 1 <= NCH + 4):
                    lo, hi = pair_cols(b, c - 1)
                    norm_factors(b * 4 + c // 2 + 1, (c // 2 + 1) % 2, lo, hi)
                b3, c3, n = at(b, c, 3)
                if valid(n) and c3 < CPB - 1:
                    pool.wait_ge(s["s_read"], 7 * b3 + c3 + 1)
                    wait_count(pool, "inter_done", 7 * b3 + c3 - 1)
                    nc.gpsimd.tensor_tensor(s_bd[:, c3 % 2, :], s_full[:], head_mask[:], ALU.mult)\
                        .then_inc(s["sbd_done"], 1)
                b8, c8, u = at(b, c, 8)
                if valid(u):
                    pool.wait_ge(s["h2T_done"], u + 1)
                    if not isinstance(b8, int) or b8 > 0:
                        pool.wait_ge(h2_stored[c8 // 4], b8 * 32)
                    nc.gpsimd.tensor_tensor(lo_w[:, c8, :], h2T_w[:, c8 % 2, :], hi_w[:, c8, :].bitcast(F32),
                                            ALU.subtract).then_inc(s["h2w_free"], 1)

            norm_factors(0, 0, 0, 2)
            made(nc.gpsimd.tensor_copy(ident_b[:], ident[:]))
            made(nc.gpsimd.memset(tri[:], 1.0))
            made(nc.gpsimd.affine_select(out=tri[:], in_=tri[:], compare_op=ALU.is_ge, fill=0.0,
                                         base=0, pattern=[[1, P]], channel_multiplier=-1))
            hm = head_mask[:].rearrange("p (h m) -> p h m", m=HV)
            made(nc.gpsimd.memset(head_mask[:], 1.0))
            made(nc.gpsimd.affine_select(out=hm, in_=hm, compare_op=ALU.is_ge, fill=0.0,
                                         base=0, pattern=[[-HD, HEADS], [0, HV]], channel_multiplier=1))
            made(nc.gpsimd.affine_select(out=hm, in_=hm, compare_op=ALU.is_ge, fill=0.0,
                                         base=HD - 1, pattern=[[HD, HEADS], [0, HV]], channel_multiplier=-1))
            made(nc.gpsimd.memset(spread[:], 1.0))
            made(nc.gpsimd.affine_select(out=spread[:], in_=spread[:], compare_op=ALU.is_equal, fill=0.0,
                                         base=0, pattern=[[-1, B], [0, P]], channel_multiplier=1))
            made(nc.gpsimd.memset(pick[:], -MASKED_OUT))
            made(nc.gpsimd.affine_select(out=pick[:], in_=pick[:], compare_op=ALU.is_equal, fill=0.0,
                                         base=0, pattern=[[2, UNITS - 1], [1, 2], [0, I]], channel_multiplier=-1))
            made(nc.gpsimd.iota(order[:], pattern=[[-1, E]], base=E, channel_multiplier=0,
                                allow_small_or_imprecise_dtypes=True))
            made(nc.gpsimd.memset(x_all[:, NCH * P:], 0.0))
            nc.gpsimd.memset(ones_f[:], 1.0).then_inc(s["const_all"], 1)

            for c in range(CPB):
                step(0, c)
            with pool.Fori(1, B) as b:
                for c in range(CPB):
                    step(b, c)
            for c in range(CPB):
                step(B, c)

            for n in range(2):
                pool.wait_ge(s["hi_done"], n + 1)
                nc.gpsimd.tensor_tensor(hid_lo[:, n, :], hid[:, n, :], hid_hi[:, n, :].bitcast(F32),
                                        ALU.subtract).then_inc(s["lo_done"], 1)

        @block.tensor
        def _(pe):
            mm = nc.tensor.matmul
            pe.wait_ge(c_loaded, 32)
            pe.wait_ge(s["const_ident"], 2)
            nc.tensor.transpose(ps_t[:, 0:B], cond_sb[:], ident[0:B, 0:B]).then_inc(s["setup_pe"], 1)
            pe.wait_ge(s["setup_dve"], 3)
            for k in (0, 1, 3, 4, 5):
                last = mm(ps_a[:, k * B:(k + 1) * B], wmod_sb[:, ts(k, D)], condT[:, 2, :], start=True, stop=True)
            last.then_inc(s["setup_pe"], 1)
            last = mm(ps_q[0:B, 0:D], condT[:, 2, :], wmod_sb[:, ts(2, D)], start=True, stop=True)
            last.then_inc(s["setup_pe"], 1)
            pe.wait_ge(s["setup_act"], 3)

            def step(b, c):
                _, c1, r = at(b, c, 1)
                if valid(r):
                    pe.wait_ge(s["hT_done"], r + 1)
                    wait_count(pe, "elu_done", r)
                    wait_count(pe, "v_done", r)
                    mm(ps_a[:, 0:3 * P], ones_b[:], bias_parts[:], start=True, stop=False)
                    mm(ps_a[:, 0:3 * P], hT[:, c1 % 2, :], w_qkv[:], start=False, stop=True)\
                        .then_inc(s["qkv_done"], 1)
                _, c3, q = at(b, c, 3)
                _, c5, v = at(b, c, 5)
                if valid(q):
                    pe.wait_ge(s["elu_done"], q + 1)
                if valid(q) or valid(v):
                    wait_count(pe, "qT_done", q, NCH)
                    wait_count(pe, "valT_done", v)
                    wait_count(pe, "x1_done", v)
                if valid(q):
                    nc.tensor.transpose(ps_q[:, 0:P], qk[:, c3 % 4, 0:P], ident[:]).then_inc(s["qT_ps"], 1)
                if valid(v):
                    pe.wait_ge(s["norm_done"], v + 1)
                    nc.tensor.transpose(ps_q[:, P:2 * P], val[:, c5 % 2, :], ident[:]).then_inc(s["valT_ps"], 1)
                _, c0, a = at(b, c, 0)
                _, c8, u = at(b, c, 8)

                def second_norm_T():
                    if not valid(u):
                        return
                    pe.wait_ge(s["xn2_done"], u + 1)
                    wait_count(pe, "hT_done", a, NCH)
                    wait_count(pe, "logits_done", u)
                    if logits_apart(b, c):
                        pe.wait_ge(s["h2T_done"], u)
                    nc.tensor.transpose(ps_t[:, 128:256], xn2[:, c8 % 2, :], ident[:]).then_inc(s["xn2T_ps"], 1)
                b3, c3, n = at(b, c, 3)
                if not valid(n) or not valid(a):
                    second_norm_T()
                if valid(n):
                    pe.wait_ge(s["kv_done"], n + 1)
                    for k, (h0, h1) in enumerate(THIRDS):
                        wait_count(pe, "qm_done", 3 * n - 2 + k)
                        w = HD * HV
                        mm(ps_c[k][:, 0:(h1 - h0) * w], tri[:], kv[:, c3 % 2, h0 * w:h1 * w],
                           start=True, stop=True).then_inc(s["C_done"], 1)
                        if k == 0 and valid(a):
                            second_norm_T()
                    if c3 < CPB - 1:
                        wait_count(pe, "s_read", 7 * b3 + c3)
                        mm(ps_s[:, 0:FV], qk[:, c3 % 4, P:2 * P], v_aug[:, c3 % 4].rearrange("p h m -> p (h m)"),
                           start=(c3 == 0), stop=True, skip_group_check=True).then_inc(s["ktv_done"], 1)
                b5, c5, m = at(b, c, 5)

                def project():
                    if not valid(m):
                        return
                    pe.wait_ge(s["valT_done"], m + 1)
                    if valid(n):
                        pe.wait_ge(s["qT_done"], n + 1)
                    pe.wait_ge(s["woga_done"], b5 + 1)
                    mm(ps_q[:, 256:384], ones_b[:], gabo_parts[:, ts(b5, D)], start=True, stop=False)
                    mm(ps_q[:, 256:384], valT[:, c5 % 2, :], w_o_ga[:], start=False, stop=False)
                    mm(ps_q[:, 256:384], ident[:], x_all[:, ts(m, P)], start=False, stop=True)\
                        .then_inc(s["y_done"], 1)

                draining = isinstance(b, int) and b == B
                if draining:
                    project()
                if valid(a):
                    pe.wait_ge(s["xn_done"], a + 1)
                    wait_count(pe, "hT_done", a)
                wait_count(pe, "logits_done", u)
                if valid(u):
                    pe.wait_ge(s["h2T_w_done"], u + 1)
                    if not logits_apart(b, c):
                        pe.wait_ge(s["h2T_done"], u + 1)
                    elif c == 1:
                        pe.wait_ge(s["elu_done"], NCH)
                        pe.wait_ge(s["v_done"], NCH)
                if valid(a):
                    nc.tensor.transpose(ps_t[:, 0:P], xn[:, c0 % 2, :], ident[:]).then_inc(s["xnT_done"], 1)
                if valid(u):
                    logits_bank = ps_a if logits_apart(b, c) else ps_t
                    mm(logits_bank[:, 256:256 + E], h2T_w[:, c8 % 2, :], rwT[:], start=True, stop=True)\
                        .then_inc(s["logits_ps"], 1)
                if not draining:
                    project()
                if valid(n) and c3 > 0:
                    pe.wait_ge(s["qT_done"], n + 1)
                    pe.wait_ge(s["sbd_done"], 7 * b3 + c3)
                    wait_count(pe, "add_done", 7 * b3 + c3 - 1)
                    mm(ps_i[:, 0:FV], qT[:, c3 % 2, :], s_bd[:, (c3 - 1) % 2, :],
                       start=True, stop=True).then_inc(s["inter_done"], 1)

            step(0, 0)
            pe.wait_ge(w_loaded, 128)
            pe.wait_ge(s["dve_const"], 1)
            pe.wait_ge(s["setup_dve"], 9)
            step(0, 1)
            pe.wait_ge(w2_loaded, 128)
            nc.tensor.transpose(ps_i[:, 384:384 + E], raw_r[:], ident[0:E, 0:E])
            for bank_, shared, raw in ((ps_c[0], 0, raw_g), (ps_c[1], 1, raw_u), (ps_c[2], 2, raw_d)):
                for u in range(UNITS):
                    src = raw[:, u, :] if raw is not raw_d else raw_d[:, ts(u, P)]
                    dst = bank_[:, ts(u, P)] if u < UNITS - 1 else ps_i[:, ts(shared, P)]
                    last = nc.tensor.transpose(dst, src, ident[:])
            last.then_inc(s["setup_pe"], 1)
            pe.wait_ge(s["const_all"], 1)
            pe.wait_ge(s["setup_dve"], 14)
            for half, bank_ in enumerate((ps_q, ps_s)):
                for b in range(4):
                    last = mm(bank_[:, ts(b, D)], spread[:, 4 * half + b, :], g8[:], start=True, stop=True)
            last.then_inc(s["setup_pe"], 1)
            step(0, 2)
            pe.wait_ge(s["setup_act"], 5)
            pe.wait_ge(s["setup_dve"], 16)
            for c in range(3, CPB):
                if c == 5:
                    pe.wait_ge(gabo_moved, 48)
                step(0, c)
            with pe.Fori(1, B) as b:
                for c in range(CPB):
                    step(b, c)
            for c in range(CPB):
                step(B, c)

            pe.wait_ge(s["qm_done"], 3 * NCH)
            pe.wait_ge(s["x1_done"], NCH)
            pe.wait_ge(s["add_done"], 7 * B)
            pe.wait_ge(s["s_read"], 7 * B)
            pe.wait_ge(s["logits_done"], NCH)
            for h in range(2):
                pe.wait_ge(h2_stored[h], 32 * (B - 1))

            def three(out_ps, w_hi, w_lo, x_hi, x_lo, start, stop):
                mm(out_ps, w_hi, x_hi, start=start, stop=False, skip_group_check=True)
                mm(out_ps, w_lo, x_hi, start=False, stop=False, skip_group_check=True)
                return mm(out_ps, w_hi, x_lo, start=False, stop=stop, skip_group_check=True)

            def gate_up(n, i, b):
                t, u = unit(i)
                j = i % 2
                tile = b * 2 + t
                x_hi = h2_hi[:, bass.ds(tile * 512, 512)]
                x_lo = h2_lo[:, bass.ds(tile * 512, 512)]
                wait_count(pe, "silu_done", n - 1)
                last = three(ps_g[j % 2][:], gw_hi[:, u, :], gw_lo[:, u, :], x_hi, x_lo, True, u == UNITS - 1)
                if u < UNITS - 1:
                    pe.wait_ge(s["selT_done"], tile + 1)
                    last = mm(ps_g[j % 2][:], pick[:, u].rearrange("e a i -> e (a i)"), selT[:, t, :],
                              start=False, stop=True, skip_group_check=True)
                last.then_inc(s["g_done"], 1)
                wait_count(pe, "hid_done", n - 1)
                three(ps_u[j % 2][:], uw_hi[:, u, :], uw_lo[:, u, :], x_hi, x_lo, True, True)\
                    .then_inc(s["u_done"], 1)

            def down(n, u, out_no, ob, j, first, last_):
                if isinstance(n, int) and n == 0:
                    pe.wait_ge(s["dwlo_done"], 1)
                pe.wait_ge(s["hi_done"], n + 1)
                if first:
                    wait_count(pe, "osb_done", out_no - 1)
                mm(ps_o[ob][:], dw_hi[:, u, :], hid_hi[:, j % 2, :], start=first, stop=False, skip_group_check=True)
                mm(ps_o[ob][:], dw_lo[:, u, :], hid_hi[:, j % 2, :], start=False, stop=False, skip_group_check=True)
                pe.wait_ge(s["lo_done"], n + 1)
                mm(ps_o[ob][:], dw_hi[:, u, :], hid_lo[:, j % 2, :], start=False, stop=last_,
                   skip_group_check=True).then_inc(s["down_done"], 1)

            def back(out_no, ob):
                pe.wait_ge(s["osb_done"], out_no + 1)
                wait_count(pe, "fin_done", out_no)
                for j in range(4):
                    last = nc.tensor.transpose(ps_x[:, ts(j, P)], o_sb[:, ob, ts(j, P)], ident[:])
                last.then_inc(s["back_done"], 1)

            def choice(no, t):
                pe.wait_ge(s["selw_done"], no + 1)
                wait_count(pe, "selT_done", no)
                for j in range(4):
                    last = nc.tensor.transpose(ps_m[:].bitcast(BF16)[0:E, ts(j, P)], sel_w[:, t, ts(j, E)], ident_b[:])
                last.then_inc(s["selT_ps"], 1)

            choice(0, 0)
            gate_up(0, 0, 0)
            choice(1, 1)
            gate_up(1, 1, 0)

            def expert_row(b, first_row, last_row):
                for i in range(UPR):
                    n = b * UPR + i
                    t, u = unit(i)
                    if first_row and i == 2:
                        pe.wait_ge(s["dwhi_done"], 1)
                        pe.wait_ge(s["dwlo_done"], 2)
                    down(n, u, b * 2 + t, t, i, u == SH, u == SH - 1)
                    if i < UPR - 2:
                        gate_up(n + 2, i + 2, b)
                    elif not last_row:
                        gate_up(n + 2, i + 2 - UPR, b + 1)
                    if first_row and i == 1:
                        pe.wait_ge(s["router"], ROUTER_OPS)
                        mm(ps_m[:, 0:2 * E], ones_f[:], tot[:], start=True, stop=True).then_inc(s["tot_ps"], 1)
                    if i == 0 and not first_row:
                        back(b * 2 - 1, 1)
                    if i == 6:
                        back(b * 2, 0)
                    if u == 2 and not last_row:
                        choice(b * 2 + 2 + t, t)

            expert_row(0, True, False)
            for h in range(2):
                pe.wait_ge(h2_stored[h], 32 * B)
            with pe.Fori(1, B - 1) as b:
                expert_row(b, False, False)
            expert_row(B - 1, False, True)
            back(TILES - 1, 1)

        @block.scalar
        def _(act):
            A = nc.scalar.activation
            act.wait_ge(s["setup_pe"], 1)
            act.wait_ge(s["dve_const"], 1)
            A(condT[:, 0, :], ps_t[:, 0:B], ACT.Exp, scale=-1.0).then_inc(s["setup_act"], 1)
            act.wait_ge(s["setup_pe"], 2)
            A(modT[:, 0:2, :].rearrange("p k b -> p (k b)"), ps_a[:, 0:2 * B], ACT.Copy)
            A(modT[:, 3:6, :].rearrange("p k b -> p (k b)"), ps_a[:, 3 * B:6 * B], ACT.Copy)\
                .then_inc(s["setup_act"], 1)
            act.wait_ge(s["setup_pe"], 3)
            A(g_raw[:], ps_q[0:B, 0:D], ACT.Copy).then_inc(s["setup_act"], 1)
            act.wait_ge(s["setup_dve"], 10)

            def xn1(b, c):
                a = b * CPB + c
                if not valid(a):
                    return
                pair = b * 4 + c // 2
                act.wait_ge(s["ln_done"], pair + 1)
                wait_count(act, "xnT_done", a - 1)
                par, col = (c // 2) % 2, c % 2
                A(xn[:, c % 2, :], x_all[:, ts(a, P)], ACT.Identity, bias=nmr[:, par, col:col + 1],
                  scale=rstd[:, par, col:col + 1]).then_inc(s["xn_done"], 1)

            def second_norm(b, c):
                b7, c7, w = at(b, c, 7)
                if not valid(w):
                    return
                j = c7 % 2
                pair = b * 4 + (c - 1) // 2 + 1 if c else b * 4
                act.wait_ge(s["ln_done"], pair + 1)
                wait_count(act, "xn2T_ps", w - 1)
                par = pair_par(c)
                A(xn2[:, j, :], x_all[:, bass.ds((2 * b * CPB + 2 * (c - 7)) * (P // 2), P)], ACT.Identity,
                  bias=nmr[:, par, 2 + j:3 + j], scale=rstd[:, par, 2 + j:3 + j]).then_inc(s["xn2_done"], 1)

            def step(b, c):
                _, c1, r = at(b, c, 1)
                if valid(r):
                    act.wait_ge(s["qkv_done"], r + 1)
                    bk_, ck_, _ = at(b, c, 5)
                    wait_count(act, "ktv_done", 7 * bk_ + min(ck_ + 1, 7))
                    wait_count(act, "kv_done", r - 3)
                    A(v_aug[:, c1 % 4, :, 0:HD], ps_a[:, 2 * P:3 * P].rearrange("p (h m) -> p h m", m=HD),
                      ACT.Copy).then_inc(s["v_done"], 1)
                    wait_count(act, "elu_done", r - 1)
                    A(e_qk[:, c1 % 2, :], ps_a[:, 0:2 * P], ACT.Exp, bias=neg1[:]).then_inc(s["exp_done"], 1)
                if not isinstance(b, int) or b > 0:
                    xn1(b, c)
                _, c3, q = at(b, c, 3)
                b5, c5, v = at(b, c, 5)
                if valid(v):
                    act.wait_ge(s["valT_ps"], v + 1)
                if valid(q):
                    act.wait_ge(s["qT_ps"], q + 1)
                    wait_count(act, "inter_done", 7 * b5 + c5)
                    A(qT[:, c3 % 2, :], ps_q[:, 0:P], ACT.Copy).then_inc(s["qT_done"], 1)
                if valid(v):
                    wait_count(act, "y_done", v - 1)
                    A(valT[:, c5 % 2, :], ps_q[:, P:2 * P], ACT.Copy).then_inc(s["valT_done"], 1)
                b8, c8, u = at(b, c, 8)
                if valid(u):
                    act.wait_ge(s["xn2T_ps"], u + 1)
                    if c8 == 0:
                        A(mod2[:], modT[:, 3:5, bass.ds(b8, 1)].rearrange("p k o -> p (k o)"), ACT.Copy)\
                            .then_inc(s["mod2_done"], 1)
                        act.wait_ge(s["mod2_done"], b8 + 1)
                    if not isinstance(b8, int) or b8 > 0:
                        act.wait_ge(h2_stored[c8 // 4], b8 * 32)
                    act.wait_ge(s["h2w_free"], u + 1)
                    A(h2T_w[:, c8 % 2, :], ps_t[:, 128:256], ACT.Identity, bias=mod2[:, 0:1],
                      scale=mod2[:, 1:2]).then_inc(s["h2T_w_done"], 1)
                    A(hi_w[:, c8, :], ps_t[:, 128:256], ACT.Identity, bias=mod2[:, 0:1],
                      scale=mod2[:, 1:2]).then_inc(s["h2T_done"], 1)
                b3, c3, n = at(b, c, 3)
                if valid(n) and c3 < CPB - 1:
                    act.wait_ge(s["ktv_done"], 7 * b3 + c3 + 1)
                    wait_count(act, "sbd_done", 7 * b3 + c3)
                    A(s_full[:], ps_s[:, 0:FV], ACT.Copy).then_inc(s["s_read"], 1)

                def attention_out():
                    if valid(v):
                        act.wait_ge(s["y_done"], v + 1)
                        A(x_all[:, bass.ds(b5 * (CPB * P) + c5 * P, P)], ps_q[:, 256:384], ACT.Copy)\
                            .then_inc(s["x1_done"], 1)

                _, c0, a = at(b, c, 0)
                if valid(a) and c == 0:
                    A(mod1[:], modT[:, 0:2, bass.ds(b, 1)].rearrange("p k o -> p (k o)"), ACT.Copy)\
                        .then_inc(s["mod1_done"], 1)
                    act.wait_ge(s["mod1_done"], b + 1)
                if not valid(a):
                    attention_out()
                    second_norm(b, c)
                if valid(u):
                    act.wait_ge(s["logits_ps"], u + 1)
                if valid(a):
                    act.wait_ge(s["xnT_done"], a + 1)
                    wait_count(act, "qkv_done", a - 1)
                    A(hT[:, c0 % 2, :], ps_t[:, 0:P], ACT.Identity, bias=mod1[:, 0:1],
                      scale=mod1[:, 1:2]).then_inc(s["hT_done"], 1)
                if valid(u):
                    logits_bank = ps_a if logits_apart(b, c) else ps_t
                    A(logits[:, ts(u, E)], logits_bank[:, 256:256 + E], ACT.Copy).then_inc(s["logits_done"], 1)
                if isinstance(b, int) and b == 0 and c < CPB - 1:
                    xn1(0, c + 1)
                if valid(a):
                    attention_out()
                    second_norm(b, c)

            xn1(0, 0)
            step(0, 0)
            step(0, 1)
            act.wait_ge(s["setup_pe"], 4)
            for hi, bank_, k in ((gw_hi, ps_c[0], 0), (uw_hi, ps_c[1], 1)):
                A(hi[:, 0:UNITS - 1, :].rearrange("p u d -> p (u d)"), bank_[:], ACT.Copy)
                A(hi[:, UNITS - 1, :], ps_i[:, ts(k, P)], ACT.Copy)
            A(dw[:, UNITS - 1, :], ps_i[:, 2 * P:3 * P], ACT.Copy)
            A(dw_hi[:, UNITS - 1, :], ps_i[:, 2 * P:3 * P], ACT.Copy)
            A(rwT[:], ps_i[:, 384:384 + E], ACT.Copy).then_inc(s["setup_act"], 1)
            A(dw[:, 0:UNITS - 1, :].rearrange("p u d -> p (u d)"), ps_c[2][:], ACT.Copy)
            act.wait_ge(s["setup_pe"], 5)
            A(ga_bc[:, 0:512], ps_q[:], ACT.Copy)
            A(ga_bc[:, 512:1024], ps_s[:], ACT.Copy).then_inc(s["setup_act"], 1)
            for c in range(2, CPB):
                step(0, c)
            with act.Fori(1, B) as b:
                for c in range(CPB):
                    step(b, c)
            def exp_of(part):
                act.wait_ge(s["router"], part * CHOICE_OPS + 1)
                cols = slice(PARTS[part] * E, PARTS[part + 1] * E)
                A(gl[1][:, cols], gl[0][:, cols], ACT.Exp, scale=-1.0).then_inc(s["logits_exp"], 1)

            for c in range(CPB):
                step(B, c)
                if c == 1:
                    exp_of(0)
            exp_of(1)
            A(gb_row[:], gbT[:, 0:1], ACT.Copy).then_inc(s["gbrow_done"], 1)

            def silu(n, j):
                act.wait_ge(s["g_done"], n + 1)
                wait_count(act, "hid_done", n - 1)
                A(silu_g[:, j % 2, :], ps_g[j % 2][:], ACT.Silu).then_inc(s["silu_done"], 1)

            def hidden_hi(n, j):
                act.wait_ge(s["hid_done"], n + 1)
                wait_count(act, "down_done", n - 1)
                A(hid_hi[:, j % 2, :], hid[:, j % 2, :], ACT.Copy).then_inc(s["hi_done"], 1)

            def out(out_no, ob, downs, gb):
                act.wait_ge(s["down_done"], downs)
                wait_count(act, "back_done", out_no if ob == 1 else out_no - 1)
                A(o_sb[:, ob, :], ps_o[ob][:], ACT.Identity, scale=gb)\
                    .then_inc(s["osb_done"], 1)

            def choice(no, t, reads):
                act.wait_ge(s["selT_ps"], no + 1)
                wait_count(act, "g_done", reads)
                A(selT[:, t, :], ps_m[0:E, 0:256].bitcast(BF16), ACT.Copy).then_inc(s["selT_done"], 1)

            choice(0, 0, 0)
            silu(0, 0)
            choice(1, 1, 0)
            silu(1, 1)

            def expert_row(b, first_row, last_row):
                for i in range(UPR):
                    n = b * UPR + i
                    t, u = unit(i)
                    if i == 1 and not first_row:
                        act.wait_ge(s["osb_done"], b * 2)
                    if first_row and i == 2:
                        act.wait_ge(s["wm_done"], 1)
                        A(dw_hi[:, 0:SH, :], dw[:, 0:SH, :], ACT.Copy).then_inc(s["dwhi_done"], 1)
                    hidden_hi(n, i)
                    if not (first_row and i == 0) and (i < UPR - 1 or not last_row):
                        silu(n + 1, i + 1)
                    if i == 0 and not first_row:
                        out(b * 2 - 1, 1, n, gb_row[:])
                    if i == 1 and not first_row:
                        A(gb_row[:], gbT[:, bass.ds(b, 1)], ACT.Copy).then_inc(s["gbrow_done"], 1)
                    if i == 6:
                        act.wait_ge(s["gbrow_done"], b + 1)
                        out(b * 2, 0, n, gb_row[:])
                    if u == 3 and not last_row:
                        choice(b * 2 + 2 + t, t, n + 1)

            expert_row(0, True, False)
            with act.Fori(1, B - 1) as b:
                expert_row(b, False, False)
            expert_row(B - 1, False, True)
            out(TILES - 1, 1, UPR * B, gb_row[:])

        @block.vector
        def _(dve):
            V = nc.vector
            V.memset(neg1[:], -1.0)
            V.memset(ones_b[:], 1.0)
            V.memset(v_aug[:], 1.0)
            V.memset(bias_parts[:], 0.0)
            V.memset(gabo_parts[:], 0.0).then_inc(s["dve_const"], 1)
            V.memset(minus_1[:], -1.0).then_inc(s["h2w_free"], 2)
            V.memset(eps[:], LN_EPS)
            V.memset(half_m[:], -0.5).then_inc(s["dve_const"], 1)
            def statistics(cols, chunks):
                for col, chunk in zip(cols, chunks):
                    V.bn_stats(st[:, col, :], x_all[:, chunk]).then_inc(s["stat_done"], 1)

            def mean_var(par, lo, hi):
                for col in range(lo, hi):
                    V.bn_aggr(agg[:, par, col, :], st[:, col, :]).then_inc(s["agg_done"], 1)

            def step(b, c):
                is_reg = not isinstance(b, int)
                no = b * CPB + c
                _, c1, r = at(b, c, 1)
                b3, c3, n = at(b, c, 3)
                b4, c4, v = at(b, c, 4)
                b5, c5, m = at(b, c, 5)

                if valid(r):
                    dve.wait_ge(s["exp_done"], r + 1)
                    wait_count(dve, "kv_done", r - 3)
                    wait_count(dve, "ktv_done", 7 * b5 + min(c5 + 1, 7))
                    wait_count(dve, "qT_ps", r - 3)
                    V.scalar_tensor_tensor(out=qk[:, c1 % 4, :], in0=e_qk[:, c1 % 2, :], scalar=1.0,
                                           in1=ps_a[:, 0:2 * P], op0=ALU.min, op1=ALU.max).then_inc(s["elu_done"], 1)

                def times_q(k):
                    if valid(n):
                        h0, h1 = THIRDS[k]
                        rows = (h1 - h0) * HD
                        dve.wait_ge(s["C_done"], 3 * n + k + 1)
                        V.tensor_tensor(prod[:, h0 * HD * HV:h1 * HD * HV].rearrange("p (r m) -> p r m", m=HV),
                                        ps_c[k][:, 0:rows * HV].rearrange("p (r m) -> p r m", m=HV),
                                        qk[:, c3 % 4, h0 * HD:h1 * HD].rearrange("p (r o) -> p r o", o=1)
                                        .broadcast_to([P, rows, HV]), ALU.mult).then_inc(s["qm_done"], 1)

                prev_pairs = c % 2 == 1 and (is_reg or b < B)
                if prev_pairs:
                    lo, hi = pair_cols(b, c - 1)
                    pair = b * 4 + (c - 1) // 2 + 1
                    dve.wait_ge(s["stat_done"], stat_before(pair) + hi - lo)
                    wait_count(dve, "ln_done", pair - 1)
                if valid(v) and c4 > 0:
                    dve.wait_ge(s["red_done"], v + 1)
                    dve.wait_ge(s["inter_done"], 7 * b4 + c4)
                    V.tensor_tensor(nd[:], ps_i[:, 0:FV], red[:], ALU.add).then_inc(s["add_done"], 1)
                if prev_pairs:
                    mean_var(((c - 1) // 2 + 1) % 2, lo, hi)
                num = (nd if c4 > 0 else red)[:].rearrange("p (h m) -> p h m", m=HV)
                wait_count(dve, "red_done", min(n, NCH) if isinstance(n, int) else n)
                times_q(0)
                if valid(v):
                    wait_count(dve, "add_done", 7 * b4 + c4)
                    wait_count(dve, "rec_done", v)
                    V.tensor_scalar(den[:], num[:, :, HD], 1e-6, None, ALU.add).then_inc(s["den_done"], 1)
                times_q(1)
                if valid(v):
                    dve.wait_ge(s["den_done"], v + 1)
                    wait_count(dve, "norm_done", v)
                    V.reciprocal(rec[:], den[:]).then_inc(s["rec_done"], 1)
                times_q(2)
                if valid(v):
                    dve.wait_ge(s["rec_done"], v + 1)
                    wait_count(dve, "valT_ps", v - 1)
                    V.tensor_tensor(val[:, c4 % 2, :].rearrange("p (h m) -> p h m", m=HD), num[:, :, 0:HD],
                                    rec[:].rearrange("p (h o) -> p h o", o=1).broadcast_to([P, HEADS, HD]),
                                    ALU.mult).then_inc(s["norm_done"], 1)

                def next_w_o_ga():
                    if valid(m) and c5 == CPB - 1 and (is_reg or b < B):
                        dve.wait_ge(s["y_done"], m + 1)
                        V.tensor_tensor(w_o_ga[:], w_o[:], ga_bc[:, ts(b, D)], ALU.mult).then_inc(s["woga_done"], 1)

                def sum_over_d():
                    if not valid(n):
                        return
                    dve.wait_ge(s["qm_done"], 3 * n + 3)
                    if c4 == 0:
                        wait_count(dve, "norm_done", n)
                    V.tensor_reduce(red[:].rearrange("p (h m) -> p h m", m=HV),
                                    prod[:].rearrange("p (h d m) -> p h m d", d=HD, m=HV), AX_X, ALU.add)\
                        .then_inc(s["red_done"], 1)

                pairs = c % 2 == 0 and (is_reg or no <= NCH + 4)
                sum_over_d()
                next_w_o_ga()
                if pairs:
                    lo, hi = pair_cols(b, c)
                    pair = b * 4 + c // 2 + 1
                    dve.wait_ge(s["agg_done"], stat_before(pair))
                    if lo == 0:
                        statistics((0, 1), (ts(no + 2, P), ts(no + 3, P)))
                    if hi == 4:
                        dve.wait_ge(s["x1_done"], no - 4)
                        statistics((2, 3), (bass.ds(no * P - 6 * P, P), bass.ds(no * P - 5 * P, P)))
                    if isinstance(b, int) and b == B:
                        dve.wait_ge(s["stat_done"], stat_before(pair) + hi - lo)
                        dve.wait_ge(s["ln_done"], pair - 1)
                        mean_var((c // 2 + 1) % 2, lo, hi)

            dve.wait_ge(x_loaded[0], 16)
            statistics((0, 1), (ts(0, P), ts(1, P)))
            dve.wait_ge(s["stat_done"], 2)
            mean_var(0, 0, 2)
            dve.wait_ge(s["setup_act"], 1)
            V.tensor_scalar(condT[:, 0, :], condT[:, 0, :], 1.0, None, ALU.add).then_inc(s["setup_dve"], 1)
            dve.wait_ge(s["setup_dve"], 1)
            V.reciprocal(condT[:, 1, :], condT[:, 0, :]).then_inc(s["setup_dve"], 1)
            dve.wait_ge(s["setup_dve"], 2)
            V.tensor_tensor(condT[:, 2, :], ps_t[:, 0:B], condT[:, 1, :], ALU.mult).then_inc(s["setup_dve"], 1)
            dve.wait_ge(w_loaded, 128)
            V.tensor_scalar(bias_row[0:1, 0:2 * P], bias_row[0:1, 0:2 * P], 1.0, None, ALU.add)\
                .then_inc(s["setup_dve"], 1)
            dve.wait_ge(s["setup_dve"], 4)
            split_row(dve, lambda k: bias_parts[32 * k:32 * k + 1, 0:3 * P], bias_row, 1, 3 * P, s["setup_dve"], 4)
            dve.wait_ge(s["setup_act"], 2)
            V.tensor_scalar(modT[:, 1, :], modT[:, 1, :], 1.0, None, ALU.add)
            V.tensor_scalar(modT[:, 4, :], modT[:, 4, :], 1.0, None, ALU.add)\
                .then_inc(s["setup_dve"], 1)
            for c in range(CPB):
                if c == 1:
                    dve.wait_ge(s["setup_act"], 3)
                    V.tensor_scalar(g_sgn[:], g_raw[:], 0.0, 2.0, ALU.is_ge, ALU.mult)
                    V.tensor_scalar(gb_sgn[:], modT[:, 5, :], 0.0, 2.0, ALU.is_ge, ALU.mult).then_inc(s["setup_dve"], 1)
                    dve.wait_ge(s["setup_dve"], 11)
                    V.tensor_scalar(g_sgn[:], g_sgn[:], -1.0, None, ALU.add)
                    V.tensor_scalar(gb_sgn[:], gb_sgn[:], -1.0, None, ALU.add).then_inc(s["setup_dve"], 1)
                    dve.wait_ge(s["setup_dve"], 12)
                    V.tensor_tensor(g_raw[:], g_raw[:], g_sgn[:], ALU.mult)
                    V.tensor_tensor(gbT[:], modT[:, 5, :], gb_sgn[:], ALU.mult).then_inc(s["setup_dve"], 1)
                    dve.wait_ge(s["setup_dve"], 13)
                    V.scalar_tensor_tensor(out=g8[:], in0=g_raw[:], scalar=0.25, in1=g_sgn[:], op0=ALU.max,
                                           op1=ALU.mult)
                    V.scalar_tensor_tensor(out=gbT[:], in0=gbT[:], scalar=0.25, in1=gb_sgn[:], op0=ALU.max,
                                           op1=ALU.mult).then_inc(s["setup_dve"], 1)
                if c == 2:
                    dve.wait_ge(s["setup_dve"], 14)
                    V.tensor_tensor(gabo[:], g8[:], bo_8[:], ALU.mult).then_inc(s["setup_dve"], 1)
                    dve.wait_ge(s["setup_dve"], 15)
                    split_row(dve, lambda k: gabo_p[:, k, :], gabo, B, D, s["gabo_split"], 0)
                    dve.wait_ge(s["setup_act"], 4)
                    for hi, lo, bank_, k in ((gw_hi, gw_lo, ps_c[0], 0), (uw_hi, uw_lo, ps_c[1], 1)):
                        V.tensor_tensor(lo[:, 0:UNITS - 1, :], bank_[:].rearrange("p (u d) -> p u d", d=P),
                                        hi[:, 0:UNITS - 1, :].bitcast(F32), ALU.subtract)
                        last = V.tensor_tensor(lo[:, UNITS - 1, :], ps_i[:, ts(k, P)],
                                               hi[:, UNITS - 1, :].bitcast(F32), ALU.subtract)
                    last.then_inc(s["setup_dve"], 1)
                if c == 3:
                    dve.wait_ge(s["const_all"], 1)
                    V.tensor_tensor(dw_lo[:, UNITS - 1, :], dw[:, UNITS - 1, :], dw_hi[:, UNITS - 1, :].bitcast(F32),
                                    ALU.subtract).then_inc(s["dwlo_done"], 1)
                    dve.wait_ge(s["setup_act"], 5)
                    V.tensor_tensor(w_o_ga[:], w_o[:], ga_bc[:, 0:D], ALU.mult).then_inc(s["woga_done"], 1)
                if c == 6:
                    dve.wait_ge(x_loaded[1], 16)
                step(0, c)
            for b in range(2, B):
                dve.wait_ge(x_loaded[b], 16)
            with dve.Fori(1, B) as b:
                for c in range(CPB):
                    step(b, c)
            steps = [0]

            def made(ins):
                ins.then_inc(s["router"], 1)
                steps[0] += 1

            def router_op(part, k):
                n0, n1 = (PARTS[part], PARTS[part + 1]) if k < CHOICE_OPS else (0, NCH)
                size = [P, n1 - n0, E]

                def g(i):
                    return gl[i][:, n0 * E:n1 * E].rearrange("p (n e) -> p n e", e=E)

                def m(i):
                    return gm[:, i, n0:n1]

                def over_e(i):
                    return m(i).rearrange("p (n o) -> p n o", o=1).broadcast_to(size)

                order_b = order[:].rearrange("p (o e) -> p o e", o=1).broadcast_to(size)
                sel = sel_m1[:, n0 * E:n1 * E]
                if k == 0:
                    dve.wait_ge(s["logits_done"], n1)
                    made(V.tensor_tensor(g(0), logits[:, n0 * E:n1 * E].rearrange("p (n e) -> p n e", e=E),
                                         lb_bc[:].rearrange("p (o e) -> p o e", o=1).broadcast_to(size), ALU.add))
                    return
                dve.wait_ge(s["router"], steps[0])
                if k == 1:
                    dve.wait_ge(s["logits_exp"], part + 1)
                    made(V.tensor_scalar(g(0), g(1), 1.0, MOST, ALU.add, ALU.min))
                if k in (2, 8):
                    made(V.tensor_reduce(m(k // 8), g(0), AX_X, ALU.min))
                if k in (3, 9):
                    made(V.tensor_tensor(g(4), g(0), over_e(k // 8), ALU.is_equal))
                if k in (4, 10):
                    made(V.tensor_tensor(g(4), g(4), order_b, ALU.mult))
                if k in (5, 11):
                    made(V.tensor_reduce(m(2 + k // 8), g(4), AX_X, ALU.max))
                if k in (6, 12):
                    made(V.tensor_tensor(g(2 + k // 8), g(4), over_e(2 + k // 8), ALU.is_equal))
                if k == 7:
                    made(V.scalar_tensor_tensor(out=g(0), in0=g(2), scalar=ABOVE, in1=g(0), op0=ALU.mult,
                                                op1=ALU.add))
                if k == 13:
                    made(V.scalar_tensor_tensor(out=sel.rearrange("p (n e) -> p n e", e=E), in0=g(2), scalar=-1.0,
                                                in1=g(3), op0=ALU.add, op1=ALU.add))
                if k == 14:
                    made(V.reciprocal(gm[:, 0:2, n0:n1], gm[:, 0:2, n0:n1]))
                if k == 15:
                    made(V.scalar_tensor_tensor(out=m(4), in0=m(0), scalar=1e-8, in1=m(1), op0=ALU.add, op1=ALU.add))
                if k == 16:
                    made(V.reciprocal(m(5), m(4)))
                if k == 17:
                    made(V.tensor_tensor(gm[:, 0:2, n0:n1], gm[:, 0:2, n0:n1],
                                         gm[:, 5:6, n0:n1].broadcast_to([P, 2, n1 - n0]), ALU.mult))
                if k == 18:
                    for i in (0, 1):
                        made(V.tensor_tensor(g(2 + i), g(2 + i), over_e(i), ALU.mult))
                if k == 19:
                    made(V.tensor_tensor(g(4), g(2), g(3), ALU.add))
                if k == 20:
                    made(V.tensor_reduce(tot[:, 0:E], gl[4][:, n0 * E:n1 * E]
                                         .rearrange("p (n e) -> p e n", e=E), AX_X, ALU.add))
                if k == 21:
                    made(V.tensor_reduce(tot[:, E:2 * E], sel.rearrange("p (n e) -> p e n", e=E), AX_X, ALU.add))

            UNTIL = (1, 1, 1, 6, 10, CHOICE_OPS, CHOICE_OPS, CHOICE_OPS)
            for c in range(CPB):
                step(B, c)
                for k in range(UNTIL[c - 1] if c else 0, UNTIL[c]):
                    router_op(0, k)
                if c == 5:
                    dve.wait_ge(s["router"], CHOICE_OPS)
                    for q in range(2):
                        V.tensor_copy(sel_w[:, q, :], sel_m1[:, ts(q, 4 * E)]).then_inc(s["selw_done"], 1)
            assert steps[0] == CHOICE_OPS

            def hidden(n, j):
                dve.wait_ge(s["silu_done"], n + 1)
                dve.wait_ge(s["u_done"], n + 1)
                wait_count(dve, "lo_done", n - 1)
                V.tensor_tensor(hid[:, j % 2, :], silu_g[:, j % 2, :], ps_u[j % 2][:], ALU.mult)\
                    .then_inc(s["hid_done"], 1)

            def finish(tile):
                dve.wait_ge(s["back_done"], tile + 1)
                xs = x_all[:, bass.ds(tile * 512, 512)]
                V.tensor_tensor(xs, xs, ps_x[:], ALU.add).then_inc(s["fin_done"], 1)

            def hidden_lo(n, j):
                dve.wait_ge(s["hi_done"], n + 1)
                wait_count(dve, "down_done", n - 1)
                wait_count(dve, "lo_done", n)
                V.tensor_tensor(hid_lo[:, j % 2, :], hid[:, j % 2, :], hid_hi[:, j % 2, :].bitcast(F32),
                                ALU.subtract).then_inc(s["lo_done"], 1)

            for k in range(CHOICE_OPS + 8):
                router_op(1, k)
                if k == 11:
                    hidden(0, 0)
                if k == 14:
                    hidden(1, 1)
            assert steps[0] == ROUTER_OPS
            dve.wait_ge(s["tot_ps"], 1)
            made(V.tensor_scalar(wmean[:, 0, :], ps_m[:, E:2 * E], float(NCH * P), 1.0, ALU.add, ALU.max))
            dve.wait_ge(s["router"], steps[0])
            made(V.reciprocal(wmean[:, 1, :], wmean[:, 0, :]))
            dve.wait_ge(s["router"], steps[0])
            made(V.tensor_tensor(wmean[:, 2, :], ps_m[:, 0:E], wmean[:, 1, :], ALU.mult))
            dve.wait_ge(s["router"], steps[0])
            pairs_ = wmean[:, 2, :].rearrange("p (u a) -> p a u", a=2)
            V.tensor_copy(wm_col[0:I, :], pairs_[0:I, 0, :])
            made(V.tensor_copy(wm_col[I:P, :], pairs_[I:P, 1, :]))
            dve.wait_ge(s["router"], steps[0])
            V.tensor_tensor(dw[:, 0:SH, :], dw[:, 0:SH, :],
                            wm_col[:].rearrange("p (u o) -> p u o", o=1).broadcast_to([P, SH, P]),
                            ALU.mult).then_inc(s["wm_done"], 1)

            def expert_row(b, first_row, last_row):
                for i in range(2 if first_row else 0, UPR):
                    n = b * UPR + i
                    t, u = unit(i)
                    if u == 0 and not last_row:
                        dve.wait_ge(s["selT_ps"], b * 2 + 1 + t)
                    hidden(n, i)
                    if first_row and i == 2:
                        dve.wait_ge(s["dwhi_done"], 1)
                        V.tensor_tensor(dw_lo[:, 0:SH, :], dw[:, 0:SH, :], dw_hi[:, 0:SH, :].bitcast(F32),
                                        ALU.subtract).then_inc(s["dwlo_done"], 1)
                    if u == 0 and not last_row:
                        no = b * 2 + 2 + t
                        V.tensor_copy(sel_w[:, t, :], sel_m1[:, bass.ds(no * (4 * E), 4 * E)])\
                            .then_inc(s["selw_done"], 1)
                    if i == 2 and not first_row:
                        finish(b * 2 - 1)
                    if i == 8:
                        finish(b * 2)
                    hidden_lo(n, i)

            expert_row(0, True, False)
            with dve.Fori(1, B - 1) as b:
                expert_row(b, False, False)
            expert_row(B - 1, False, True)
            finish(TILES - 1)


_INS = ['L0_attn_x', 'L0_attn_Wq', 'L0_attn_bq', 'L0_attn_Wk', 'L0_attn_bk', 'L0_attn_Wv', 'L0_attn_bv',
        'L0_attn_Wo', 'L0_attn_bo', 'L0_ffn_gate_w', 'L0_ffn_lb_bias', 'L0_ffn_expert_gate_w',
        'L0_ffn_expert_up_w', 'L0_ffn_expert_down_w', 'L0_ffn_shared_gate_w', 'L0_ffn_shared_up_w',
        'L0_ffn_shared_down_w', 'L0_c', 'L0_wmod']
_OUTS = [((8, 1024, 128), 'float32')]


def kernel(**inputs):
    import numpy as _np
    import concourse.bacc as _bacc
    from concourse import mybir as _mybir
    from concourse.bass_utils import run_bass_kernel_spmd as _run

    nc = _bacc.Bacc("TRN2", target_bir_lowering=False, num_devices=1)
    arrays, args = {}, []
    for name in _INS:
        a = _np.ascontiguousarray(inputs[name])
        arrays[f"in_{name}_dram"] = a
        args.append(nc.dram_tensor(f"in_{name}_dram", a.shape, _mybir.dt.from_np(a.dtype), kind="ExternalInput").ap())
    for i, (shape, dtype) in enumerate(_OUTS):
        dt = _mybir.dt.from_np(_np.dtype(dtype))
        args.append(nc.dram_tensor(f"out_{i}_dram", shape, dt, kind="ExternalOutput").ap())
    adaln_block(nc, *args)
    r = _run(nc, [arrays], core_ids=[0])
    got = tuple(r.results[0][f"out_{i}_dram"] for i in range(len(_OUTS)))
    return got[0]
```
